# Optimizing a Trainium2 kernel written in Bass

```python
import numpy as np
import jax
import jax.numpy as jnp

def _softmax(x, axis=-1):
    return jax.nn.softmax(x, axis=axis)

def _gelu(x):
    return jax.nn.gelu(x, approximate=True)

def _silu(x):
    return jax.nn.silu(x)

def _sigmoid(x):
    return jax.nn.sigmoid(x)

def _layernorm(x, axis=-1, eps=1e-05):
    m = jnp.mean(x, axis=axis, keepdims=True)
    v = jnp.var(x, axis=axis, keepdims=True)
    return (x - m) / jnp.sqrt(v + eps)

def _scatter_add(tgt, idx, src, axis=0):
    return tgt.at[idx].add(src)

def _segment_sum(src, seg, n):
    return jax.ops.segment_sum(src, seg, n)
kernel_name = 'mk_vit_tower_d1_tok_img4096_r4_5c1ca8'

def setup_inputs(seed: int=0):
    np.random.seed(seed)
    _w = jnp.asarray

    def _rec_inputs():
        import jax
        import jax.numpy as jnp
        _rk = jax.random.key(seed)
        x = -0.0064186 + 0.999588 * jax.random.normal(jax.random.fold_in(_rk, 1), (64, 128, 64, 2), jnp.float32)
        return x
    x = _rec_inputs()

    def _L0_tok_setup():
        import jax, jax.numpy as jnp
        import numpy as np
        import math
        H, N, C, L_VAL = (128, 64, 1, 1024)
        EPS = 1e-07

        def _reciprocal(x, epsilon):
            xc = jnp.conj(x)
            return xc / (x * xc + epsilon)
        key = jax.random.key(seed)
        k1, k2, k3 = jax.random.split(key, 3)
        log_dt = math.log(0.001) + jax.random.uniform(k1, (H,), dtype=jnp.float32) * (math.log(0.1) - math.log(0.001))
        log_dt = jnp.tile(log_dt[:, None], (1, 2))
        lam_im = jax.random.normal(k2, (N,), dtype=jnp.float32)
        Lambda = jnp.stack([-0.5 * jnp.ones((N,), jnp.float32), lam_im], axis=-1)
        W = jax.random.normal(k3, (C, H, N, 2), dtype=jnp.float32)
        return {'log_dt': log_dt, 'Lambda': Lambda, 'W': W, 'L': L_VAL}
    _L0_tok_all = _L0_tok_setup()
    _L0_tok_in = {k: v for k, v in _L0_tok_all.items() if k in ('log_dt', 'Lambda')}
    del _L0_tok_all

    def _L0_attn_setup():
        import jax, jax.numpy as jnp
        import numpy as np
        import math
        B, T, D_IN, D_OUT = (2, 512, 1024, 1024)
        N_HEADS, N_KV = (32, 8)
        HEAD_DIM = D_OUT // N_HEADS
        GROUP_SIZE = N_HEADS // N_KV
        ROPE_BASE = 500000.0
        CTX = 512

        def _rope_tables(head_dim, base, seq_len):
            inv_freq = 1.0 / base ** (jnp.arange(0, head_dim, 2, dtype=jnp.float32) / head_dim)
            t = jnp.arange(seq_len, dtype=jnp.float32)
            freqs = jnp.einsum('i,j->ij', t, inv_freq)
            return (jnp.cos(freqs), jnp.sin(freqs))

        def _apply_rope(x, cos, sin):
            x1, x2 = jnp.split(x, 2, axis=-1)
            c = cos[None, None]
            s = sin[None, None]
            return jnp.concatenate([x1 * c - x2 * s, x1 * s + x2 * c], axis=-1)
        key = jax.random.key(seed)
        ks = jax.random.split(key, 5)
        scale = 0.02
        return {'x': jax.random.normal(ks[0], (B, T, D_IN), dtype=jnp.float32), 'Wq': jax.random.normal(ks[1], (D_IN, D_OUT), dtype=jnp.float32) * scale, 'Wk': jax.random.normal(ks[2], (D_IN, N_KV * HEAD_DIM), dtype=jnp.float32) * scale, 'Wv': jax.random.normal(ks[3], (D_IN, N_KV * HEAD_DIM), dtype=jnp.float32) * scale, 'Wo': jax.random.normal(ks[4], (D_OUT, D_OUT), dtype=jnp.float32) * scale}
    _L0_attn_all = _L0_attn_setup()
    _L0_attn_in = {k: v for k, v in _L0_attn_all.items() if k in ('Wq', 'Wk', 'Wv', 'Wo')}
    del _L0_attn_all

    def _L0_ffn_setup():
        import jax, jax.numpy as jnp
        import numpy as np
        ALPHA = 32
        R = 16
        SCALING = ALPHA / R
        key = jax.random.key(seed)
        k1, k2, k3, k4 = jax.random.split(key, 4)
        B_, S, D = (4, 512, 1024)
        H, r, O = (8, R, 1024)
        x = jax.random.normal(k1, (B_, S, D), dtype=jnp.float32)
        A = jax.random.normal(k2, (H, r, D), dtype=jnp.float32) * 0.02
        Bm = jax.random.normal(k3, (H, O, r), dtype=jnp.float32) * 0.02
        Wr = jax.random.normal(k4, (H, D), dtype=jnp.float32) * 0.02
        br = jnp.zeros((H,), dtype=jnp.float32)
        return {'x': x, 'A': A, 'B': Bm, 'Wr': Wr, 'br': br}
    _L0_ffn_all = _L0_ffn_setup()
    _L0_ffn_in = {k: v for k, v in _L0_ffn_all.items() if k in ('A', 'B', 'Wr', 'br')}
    del _L0_ffn_all
    return {'x': x, 'L0_tok_log_dt': _L0_tok_in['log_dt'], 'L0_tok_Lambda': _L0_tok_in['Lambda'], 'L0_attn_Wq': _L0_attn_in['Wq'], 'L0_attn_Wk': _L0_attn_in['Wk'], 'L0_attn_Wv': _L0_attn_in['Wv'], 'L0_attn_Wo': _L0_attn_in['Wo'], 'L0_ffn_A': _L0_ffn_in['A'], 'L0_ffn_B': _L0_ffn_in['B'], 'L0_ffn_Wr': _L0_ffn_in['Wr'], 'L0_ffn_br': _L0_ffn_in['br']}

def reference(x, L0_tok_log_dt, L0_tok_Lambda, L0_attn_Wq, L0_attn_Wk, L0_attn_Wv, L0_attn_Wo, L0_ffn_A, L0_ffn_B, L0_ffn_Wr, L0_ffn_br):
    import jax
    import jax.numpy as jnp

    def _L0_tok_ref(log_dt, Lambda, W, L):
        import jax, jax.numpy as jnp
        import numpy as np
        import math
        H, N, C, L_VAL = (128, 64, 1, 1024)
        EPS = 1e-07

        def _reciprocal(x, epsilon):
            xc = jnp.conj(x)
            return xc / (x * xc + epsilon)
        Lam = Lambda[:, 0] + 1j * Lambda[:, 1]
        Wc = W[..., 0] + 1j * W[..., 1]
        dt = jnp.exp(log_dt)
        dt_Lambda = dt[:, None, 0] * Lambda[None, :, 0] + 1j * (dt[:, None, 1] * Lambda[None, :, 1])
        pos = jnp.arange(L, dtype=jnp.float32)
        gt0 = (Lam.real > 0).astype(dt_Lambda.real.dtype)
        P_max = jax.lax.stop_gradient(dt_Lambda * (gt0 * (L - 1)))
        dt_Lambda_neg = dt_Lambda * (1 - 2 * gt0)
        num = jnp.exp(dt_Lambda_neg) - 1
        den = jnp.exp(dt_Lambda_neg * L) - 1
        Wc = Wc * num * _reciprocal(den * Lam, EPS)
        P = dt_Lambda[..., None] * pos - P_max[..., None]
        K = jnp.einsum('chn,hnl->chl', Wc, jnp.exp(P))
        return K.real.astype(jnp.float32)

    def _L0_attn_ref(x, Wq, Wk, Wv, Wo):
        import jax, jax.numpy as jnp
        import numpy as np
        import math
        B, T, D_IN, D_OUT = (2, 512, 1024, 1024)
        N_HEADS, N_KV = (32, 8)
        HEAD_DIM = D_OUT // N_HEADS
        GROUP_SIZE = N_HEADS // N_KV
        ROPE_BASE = 500000.0
        CTX = 512

        def _rope_tables(head_dim, base, seq_len):
            inv_freq = 1.0 / base ** (jnp.arange(0, head_dim, 2, dtype=jnp.float32) / head_dim)
            t = jnp.arange(seq_len, dtype=jnp.float32)
            freqs = jnp.einsum('i,j->ij', t, inv_freq)
            return (jnp.cos(freqs), jnp.sin(freqs))

        def _apply_rope(x, cos, sin):
            x1, x2 = jnp.split(x, 2, axis=-1)
            c = cos[None, None]
            s = sin[None, None]
            return jnp.concatenate([x1 * c - x2 * s, x1 * s + x2 * c], axis=-1)
        b, t, _ = x.shape
        cos, sin = _rope_tables(HEAD_DIM, ROPE_BASE, t)
        q = (x @ Wq).reshape(b, t, N_HEADS, HEAD_DIM).transpose(0, 2, 1, 3)
        k = (x @ Wk).reshape(b, t, N_KV, HEAD_DIM).transpose(0, 2, 1, 3)
        v = (x @ Wv).reshape(b, t, N_KV, HEAD_DIM).transpose(0, 2, 1, 3)
        q = _apply_rope(q, cos, sin)
        k = _apply_rope(k, cos, sin)
        k_h = jnp.repeat(k, GROUP_SIZE, axis=1)
        v_h = jnp.repeat(v, GROUP_SIZE, axis=1)
        scores = jnp.einsum('bhqd,bhkd->bhqk', q, k_h) / math.sqrt(HEAD_DIM)
        causal = jnp.triu(jnp.ones((t, t), dtype=bool), k=1)
        scores = jnp.where(causal[None, None], jnp.finfo(scores.dtype).min, scores)
        attn = jax.nn.softmax(scores, axis=-1)
        ctx = jnp.einsum('bhqk,bhkd->bhqd', attn, v_h)
        ctx = ctx.transpose(0, 2, 1, 3).reshape(b, t, D_OUT)
        return ctx @ Wo

    def _L0_ffn_ref(x, A, B, Wr, br):
        import jax, jax.numpy as jnp
        import numpy as np
        ALPHA = 32
        R = 16
        SCALING = ALPHA / R
        H = A.shape[0]
        router_logits = jnp.einsum('bsd,hd->bsh', x, Wr) + br
        scores = H * jax.nn.softmax(router_logits, axis=-1)
        low = jnp.einsum('bsd,hrd->bshr', x, A)
        out = jnp.einsum('bshr,hor,bsh->bso', low, B, scores)
        return SCALING * out
    h = _L0_tok_ref(L0_tok_log_dt, L0_tok_Lambda, x, 1024)
    h = h + _L0_attn_ref(_layernorm(h, axis=-1), L0_attn_Wq, L0_attn_Wk, L0_attn_Wv, L0_attn_Wo)
    h = h + _L0_ffn_ref(_layernorm(h, axis=-1), L0_ffn_A, L0_ffn_B, L0_ffn_Wr, L0_ffn_br)
    return h

_drawn_inputs = setup_inputs


def setup_inputs(seed=0):
    import zlib

    import numpy as np

    out = dict(_drawn_inputs(seed))
    spreads = {'L0_ffn_br': (0.0, 0.1)}
    factors = {}
    for name, (base, spread) in spreads.items():
        noise = np.random.default_rng([zlib.crc32(name.encode()), seed]).standard_normal(out[name].shape)
        drawn = base * np.exp(spread * noise) if base else spread * noise
        out[name] = jnp.asarray(drawn.astype(out[name].dtype))
    for name, factor in factors.items():
        out[name] = (out[name] * factor).astype(out[name].dtype)
    return out
```

```python
from contextlib import ExitStack

import concourse.bass as bass
import numpy as np
from concourse import mybir

f32 = mybir.dt.float32
f16 = mybir.dt.float16
ALU = mybir.AluOpType
ACT = mybir.ActivationFunctionType
AX = mybir.AxisListType

P = 128
NB = 64
T = 128
D = 1024
NS = 64
H, G, HD = 32, 8, 32
HG = H // G
KC = D // P
NF, R = 8, 16
AW = NF * R + NF
WS = 64.0
INV_WS = 1.0 / WS
LN_EPS = 1e-5
RECIP_EPS = 1e-7
SEG = 32
FFN_SCALE = 2.0 * NF
ROPE_BASE = 500000.0

TC = 16
CHUNKS = T // TC
PAIRS = TC // 2
MAGIC = 12582912.0
INV_2PI = 0.15915494309189535
TWO_PI_HI = 6.28125
TWO_PI_LO = 2.0 * float(np.pi) - 6.28125
PI_SAFE = 3.1415925

C_IDENT, C_MASK = 0, 128
C_QC, C_QS, C_KC, C_KS = 256, 288, 320, 352
C_POS, C_END, C_EVEN, C_ODD, C_NEVEN = 384, 448, 450, 451, 452
C_N = 453


def constants():
    c = np.zeros((P, C_N), np.float32)
    c[:, C_IDENT:C_IDENT + P] = np.eye(P, dtype=np.float32)
    c[:, C_MASK:C_MASK + P] = np.triu(np.full((P, P), 1e30, np.float32), k=1)
    inv_freq = (1.0 / np.float32(ROPE_BASE) ** (np.arange(0, HD, 2, dtype=np.float32) / HD)).astype(np.float32)
    freqs = np.arange(T, dtype=np.float32)[:, None] * inv_freq[None]
    cos, sin = np.cos(freqs).astype(np.float64), np.sin(freqs).astype(np.float64)
    for at_c, at_s, s in ((C_QC, C_QS, -INV_WS / np.sqrt(HD)), (C_KC, C_KS, INV_WS)):
        c[:, at_c:at_c + HD] = np.concatenate([cos, cos], 1) * s
        c[:, at_s:at_s + HD] = np.concatenate([-sin, sin], 1) * s
    c[:, C_POS:C_POS + SEG] = np.arange(0, D, SEG)
    c[:, C_POS + SEG:C_POS + 2 * SEG] = np.arange(SEG)
    c[:, C_END] = -(D - SEG)
    c[:, C_END + 1] = -(SEG - 1)
    c[0::2, C_EVEN] = 1.0
    c[1::2, C_ODD] = 1.0
    c[0::2, C_NEVEN] = -1.0
    return c


def vit_layer(nc, x, log_dt, lam, wq, wk, wv, wo, fa, fb, wr, br, consts, h0, out):
    with ExitStack() as keep:
        def sbk(name, shape, dt=f32):
            return keep.enter_context(nc.sbuf_tensor(name, shape, dt))

        W = {
            "cst": sbk("cst", [P, C_N]),
            "ident16": sbk("ident16", [P, P], f16),
            "br_all": sbk("br_all", [P, NF]),
            "wq_hi": sbk("wq_hi", [P, KC, D], f16), "wq_lo": sbk("wq_lo", [P, KC, D], f16),
            "wo_hi": sbk("wo_hi", [P, KC, D], f16), "wo_lo": sbk("wo_lo", [P, KC, D], f16),
            "wkv_hi": sbk("wkv_hi", [P, KC, 512], f16), "wkv_lo": sbk("wkv_lo", [P, KC, 512], f16),
            "aw_hi": sbk("aw_hi", [P, KC, AW], f16), "aw_lo": sbk("aw_lo", [P, KC, AW], f16),
            "bm_hi": sbk("bm_hi", [P, D], f16), "bm_lo": sbk("bm_lo", [P, D], f16),
        }
        s4_stage(nc, x, log_dt, lam, wq, wk, wv, wo, fa, fb, wr, br, consts, h0, W)
        layer_stage(nc, h0, out, W)


def s4_stage(nc, x, log_dt, lam, wq, wk, wv, wo, fa, fb, wr, br, consts, h0, W):
    with ExitStack() as ctx:
        def sb(name, shape, dt=f32):
            return ctx.enter_context(nc.sbuf_tensor(name, shape, dt))

        def sem(name):
            return ctx.enter_context(nc.semaphore(name))

        cst = W["cst"]
        ident = cst[:, C_IDENT:C_IDENT + P]
        even, odd, neven = (cst[:, c:c + 1] for c in (C_EVEN, C_ODD, C_NEVEN))

        z = [[[sb(f"z{i}{j}{k}", [P, D]) for k in range(2)] for j in range(2)] for i in range(2)]

        def part(buf, at, n):
            return buf[:, at:at + n]

        def two(buf, at):
            return buf[:, at:at + 2 * T].rearrange("p (a t) -> p a t", a=2)

        lam_p = sb("lam_p", [P, 2])
        gt0 = sb("gt0", [P, 1])
        sgn = sb("sgn", [P, 1])
        off = sb("off", [P, 2])
        pos = sb("pos", [P, 2 * SEG])
        zr = sb("zr", [P, T])
        zi = sb("zi", [P, T])
        rr = sb("rr", [P, T])
        ss = sb("ss", [P, T])
        b0, b1, b2, b3 = z[0][0][0], z[0][0][1], z[0][1][0], z[1][0][0]
        ldt, dt = part(b0, 0, 2 * T), part(b0, 2 * T, 2 * T)
        xr, yi = two(b0, 4 * T), two(b0, 6 * T)
        pk, pf, tau, sy = (two(b1, 2 * T * i) for i in range(4))
        hy, nd_r, nd_i, em = (two(b2, 2 * T * i) for i in range(4))
        t0, t1, dr, di, gr, gi, q0, q1 = (part(b3, T * i, T) for i in range(8))
        t2, dden = two(z[1][0][1], 0), two(z[1][0][1], 2 * T)
        fa_st, wr_st = z[0][0][0], z[0][1][0]
        fb_st = z[0][0][1][:, :].rearrange("p (k q) -> p k q", k=KC)

        theta = sb("theta", [P, TC, 2 * SEG])
        expo = sb("expo", [P, TC, 2 * SEG])
        turns = sb("turns", [P, TC, 2 * SEG])
        half = sb("half", [P, TC, 2 * SEG])
        m1, m2, m3, m4 = (sb(f"m{i}", [P, TC, SEG]) for i in range(4))
        tab_r = [sb(f"tab_r{i}", [P, TC, 2 * SEG]) for i in range(2)]
        tab_i = [sb(f"tab_i{i}", [P, TC, 2 * SEG]) for i in range(2)]
        u_r = [sb(f"u_r{i}", [P, TC, SEG]) for i in range(2)]
        u_i = [sb(f"u_i{i}", [P, TC, SEG]) for i in range(2)]

        xq = [sb(f"xq{i}", [P, PAIRS, P]) for i in range(2)]
        xt = [sb(f"xt{i}", [P, 4 * P]) for i in range(2)]
        hout = [sb(f"hout{i}", [P, D]) for i in range(2)]
        wst = [sb(f"wst{i}", [P, D]) for i in range(2)]

        hps = [[ctx.enter_context(nc.psum_tensor(f"hps{i}{j}", [P, 512], f32)) for j in range(2)] for i in range(2)]
        xps = [ctx.enter_context(nc.psum_tensor(f"xps{i}", [P, 4 * P], f32)) for i in range(2)]
        fps = [ctx.enter_context(nc.psum_tensor(f"fps{i}", [P, 4 * P], f32)) for i in range(2)]

        small_in = sem("small_in")
        pre_v = sem("pre_v")
        pre_a = sem("pre_a")
        x_in = [sem(f"x_in{i}") for i in range(2)]
        w_in = [sem(f"w_in{i}") for i in range(2)]
        w_hi = sem("w_hi")
        w_lo = sem("w_lo")
        ffn_in = sem("ffn_in")
        ffn_t = sem("ffn_t")
        ffn_hi = sem("ffn_hi")
        ffn_lo = sem("ffn_lo")
        tab_v = sem("tab_v")
        tab_a = sem("tab_a")
        tab_p = sem("tab_p")
        z_v = sem("z_v")
        z_p = sem("z_p")
        z_used = sem("z_used")
        h_copied = sem("h_copied")
        xt_ps = sem("xt_ps")
        xt_sb = sem("xt_sb")
        h_sent = [sem(f"h_sent{i}") for i in range(2)]

        TV, TA, TP = 11, 4, 5
        x_v = x.rearrange("c (j s) n r -> s c j (n r)", s=2)
        h_v = h0.rearrange("c (j s) l -> s c j l", s=2)
        W_ITEMS = (("wq", D), ("wo", D), ("wkv", 512))
        W_COUNT = (16, 16, 48, 32, 64, 64)

        def ffn_parts(n, which):
            if n == 2:
                return (W["aw_" + which][:, :, P:AW],
                        fps[0][:, 0:KC * NF].rearrange("p (k h) -> p k h", k=KC))
            if n < 2:
                return (W["aw_" + which][:, 4 * n:4 * n + 4, 0:P],
                        fps[n][:, :].rearrange("p (k h) -> p k h", k=4))
            return W["bm_" + which][:, 512 * (n - 3):512 * (n - 2)], fps[n % 2][:, :]

        with nc.Block() as block:
            @block.sync
            def _(sp):
                sp.dma_start(ldt, log_dt.rearrange("t r -> (t r)").partition_broadcast(P)).then_inc(small_in, 16)
                for r in range(2):
                    sp.dma_start(lam_p[r:P:2, :], lam).then_inc(small_in, 16)
                sp.dma_start(cst[:, :], consts).then_inc(small_in, 16)
                sp.dma_start(W["br_all"][:, :], br.partition_broadcast(P)).then_inc(small_in, 16)
                for i in range(2):
                    sp.sem_inc(h_sent[i], 32)

                def load_x(k, ring):
                    for s in range(2):
                        sp.dma_start(xq[ring][64 * s:64 * s + 64, :, :],
                                     x_v[s, :, bass.ds(k * PAIRS, PAIRS), :]).then_inc(x_in[ring], 16)

                def chunk(cc, h, last):
                    k = 2 * cc + h
                    if not last:
                        sp.wait_ge(xt_ps, 2 * k + 1)
                        load_x(k + 1, (h + 1) % 2)
                    rows = bass.ds(k * P, P)
                    srcs = (((0, wq),), ((0, wo),), ((0, wk), (256, wv)))
                    for j in range(PAIRS):
                        if j in (0, 2, 4):
                            n = j // 2
                            sp.wait_ge(w_lo, 3 * k + n + 1)
                            ring = (3 * h + n) % 2
                            for at, src in srcs[n]:
                                sp.dma_start(wst[ring][:, at:at + src.shape[1]],
                                             src[rows, :]).then_inc(w_in[ring], 16)
                        pair = k * PAIRS + j
                        sp.wait_ge(h_copied, 2 * pair + 6)
                        for s in range(2):
                            sp.dma_start(h_v[s, :, bass.ds(pair, 1), :].rearrange("c j l -> c (j l)"),
                                         hout[j % 2][64 * s:64 * s + 64, :]).then_inc(h_sent[j % 2], 16)

                load_x(0, 0)
                with sp.Fori(0, CHUNKS // 2 - 1) as cc:
                    chunk(cc, 0, False)
                    chunk(cc, 1, False)
                chunk(CHUNKS // 2 - 1, 0, False)
                chunk(CHUNKS // 2 - 1, 1, True)
                sp.wait_ge(z_used, T // 2 + 2)
                sp.dma_start(fa_st[:, :], fa.rearrange("h r d -> (h r) d")).then_inc(ffn_in, 16)
                sp.dma_start(wr_st[0:NF, :], wr).then_inc(ffn_in, 16)
                for h in range(NF):
                    sp.dma_start(fb_st[:, :, h * R:(h + 1) * R],
                                 fb[h].rearrange("(k p) r -> p k r", p=P)).then_inc(ffn_in, 16)
                for i in range(2):
                    sp.wait_ge(h_sent[i], 32 * (T // 4) + 32)

            @block.gpsimd
            def _(pool):
                pool.sem_inc(z_p, 1)
                pool.wait_ge(pre_v, N_PRE)

                def exponents(k):
                    nc.gpsimd.tensor_tensor(expo[:, :, :],
                                            zr[:, bass.ds(k * TC, TC)].unsqueeze(2).broadcast_to([P, TC, 2 * SEG]),
                                            pos[:, :].unsqueeze(1).broadcast_to([P, TC, 2 * SEG]),
                                            ALU.mult).then_inc(tab_p, 1)

                def table_i(k, ring, first):
                    pool.wait_ge(tab_a, TA * k + 3)
                    if not first:
                        pool.wait_ge(z_v, (k - 1) * PAIRS + 1)
                    nc.gpsimd.tensor_tensor(tab_i[ring][:, :, :], expo[:, :, :], theta[:, :, :],
                                            ALU.mult).then_inc(tab_p, 1)

                def digits_i(k, ring):
                    rr_b, ss_b = (a[:, bass.ds(k * TC, TC)].unsqueeze(2).broadcast_to([P, TC, SEG]) for a in (rr, ss))
                    pool.wait_ge(tab_v, TV * k + 8)
                    nc.gpsimd.tensor_tensor(m3[:, :, :], ss_b, tab_r[ring][:, :, 0:SEG], ALU.mult).then_inc(tab_p, 1)
                    pool.wait_ge(tab_p, TP * k + 2)
                    nc.gpsimd.tensor_tensor(m4[:, :, :], rr_b, tab_i[ring][:, :, 0:SEG], ALU.mult).then_inc(tab_p, 1)
                    pool.wait_ge(tab_p, TP * k + 4)
                    nc.gpsimd.tensor_tensor(u_i[ring][:, :, :], m3[:, :, :], m4[:, :, :],
                                            ALU.subtract).then_inc(tab_p, 1)

                def summand(k, j, ring):
                    pool.wait_ge(z_used, k * PAIRS + j + 1)
                    if j == 0:
                        pool.wait_ge(tab_p, TP * k + 5)
                    nc.gpsimd.tensor_tensor(
                        z[j % 2][1][1][:, :].rearrange("p (a b) -> p a b", a=SEG),
                        u_i[ring][:, 2 * j + 1, :].unsqueeze(2).broadcast_to([P, SEG, SEG]),
                        tab_i[ring][:, 2 * j + 1, SEG:].unsqueeze(1).broadcast_to([P, SEG, SEG]),
                        ALU.mult).then_inc(z_p, 1)

                def chunk(cc, h, last):
                    k = 2 * cc + h
                    for j in range(PAIRS):
                        if j == 0 and not last:
                            exponents(k + 1)
                        if j == 4 and not last:
                            table_i(k + 1, (h + 1) % 2, False)
                        if j == 5 and not last:
                            digits_i(k + 1, (h + 1) % 2)
                        summand(k, j, h)

                exponents(0)
                table_i(0, 0, True)
                digits_i(0, 0)
                with pool.Fori(0, CHUNKS // 2 - 1) as cc:
                    chunk(cc, 0, False)
                    chunk(cc, 1, False)
                chunk(CHUNKS // 2 - 1, 0, False)
                chunk(CHUNKS // 2 - 1, 1, True)

            @block.scalar
            def _(act):
                act.sem_inc(h_copied, 4)
                act.sem_inc(xt_sb, 2)
                act.wait_ge(small_in, 80)
                nc.scalar.activation(dt, ldt, ACT.Exp).then_inc(pre_a, 1)
                act.wait_ge(pre_v, V_X)
                nc.scalar.activation(tau, xr, ACT.Tanh, scale=0.5).then_inc(pre_a, 1)
                act.wait_ge(pre_v, V_F)
                nc.scalar.activation(sy, pf, ACT.Sin).then_inc(pre_a, 1)
                nc.scalar.activation(hy, pf, ACT.Sin, scale=0.5).then_inc(pre_a, 1)

                def exps(k):
                    act.wait_ge(tab_p, TP * k + 1)
                    nc.scalar.activation(expo[:, :, :], expo[:, :, :], ACT.Exp).then_inc(tab_a, 1)

                def sines(k):
                    act.wait_ge(tab_v, TV * k + 6)
                    nc.scalar.activation(half[:, :, :], theta[:, :, :], ACT.Sin, scale=0.5).then_inc(tab_a, 1)
                    act.wait_ge(tab_a, TA * k + 2)
                    nc.scalar.activation(theta[:, :, :], theta[:, :, :], ACT.Sin).then_inc(tab_a, 1)
                    nc.scalar.activation(half[:, :, :], half[:, :, :], ACT.Square).then_inc(tab_a, 1)

                def weight_hi(cc, h, n):
                    k, ring = 2 * cc + h, (3 * h + n) % 2
                    name, width = W_ITEMS[n]
                    act.wait_ge(w_in[ring], 64 * cc + W_COUNT[3 * h + n])
                    nc.scalar.activation(W[name + "_hi"][:, bass.ds(k, 1), :].rearrange("p k n -> p (k n)"),
                                         wst[ring][:, 0:width], ACT.Copy, scale=WS).then_inc(w_hi, 1)

                def copy_xt(t, half_):
                    act.wait_ge(xt_ps, t + 1)
                    nc.scalar.activation(xt[half_][:, :], xps[half_][:, :], ACT.Copy).then_inc(xt_sb, 1)

                def chunk(cc, h, last):
                    k = 2 * cc + h
                    for j in range(PAIRS):
                        if j == 0:
                            copy_xt(2 * k + 1, 1)
                        if j == 4 and not last:
                            copy_xt(2 * k + 2, 0)
                        if j == 1 and not last:
                            exps(k + 1)
                        if j == 2 and not last:
                            sines(k + 1)
                        if j in (1, 3, 5):
                            weight_hi(cc, h, j // 2)
                        pair = k * PAIRS + j
                        act.wait_ge(z_used, pair + 3)
                        act.wait_ge(h_sent[j % 2], 32 * (k * PAIRS // 2 + j // 2) + 32)
                        for n in range(2):
                            nc.scalar.activation(hout[j % 2][:, n * 512:n * 512 + 512], hps[j % 2][n][:, :],
                                                 ACT.Copy).then_inc(h_copied, 1)

                exps(0)
                sines(0)
                copy_xt(0, 0)
                with act.Fori(0, CHUNKS // 2 - 1) as cc:
                    chunk(cc, 0, False)
                    chunk(cc, 1, False)
                chunk(CHUNKS // 2 - 1, 0, False)
                chunk(CHUNKS // 2 - 1, 1, True)
                for n in range(5):
                    act.wait_ge(ffn_t, n + 1)
                    dst, src = ffn_parts(n, "hi")
                    nc.scalar.activation(dst, src, ACT.Copy, scale=WS).then_inc(ffn_hi, 1)

            @block.vector
            def _(dve):
                steps = [0]

                def step(ins):
                    steps[0] += 1
                    ins.then_inc(pre_v, 1)
                    dve.wait_ge(pre_v, steps[0])

                V = nc.vector
                dve.sem_inc(z_v, 1)
                dve.sem_inc(w_lo, 2)
                dve.wait_ge(small_in, 80)
                step(V.tensor_copy(W["ident16"][:, :], ident))
                step(V.tensor_scalar(gt0[:, :], lam_p[:, 0:1], 0.0, None, ALU.is_gt))
                step(V.tensor_scalar(sgn[:, :], gt0[:, :], -2.0, 1.0, ALU.mult, ALU.add))
                step(V.tensor_scalar(off[:, :], cst[:, C_END:C_END + 2], gt0[:, :], None, ALU.mult))
                for d in range(2):
                    step(V.tensor_scalar(pos[:, d * SEG:(d + 1) * SEG], cst[:, C_POS + d * SEG:C_POS + (d + 1) * SEG],
                                         off[:, d:d + 1], None, ALU.add))
                dve.wait_ge(pre_a, 1)
                dt_v = dt.rearrange("p (t r) -> p t r", r=2)
                step(V.tensor_scalar(zr[:, :], dt_v[:, :, 0], lam_p[:, 0:1], None, ALU.mult))
                step(V.tensor_scalar(zi[:, :], dt_v[:, :, 1], lam_p[:, 1:2], None, ALU.mult))
                for n, length in enumerate((1.0, float(D))):
                    step(V.tensor_scalar(xr[:, n, :], zr[:, :], sgn[:, :], length, ALU.mult, ALU.mult))
                    step(V.tensor_scalar(yi[:, n, :], zi[:, :], sgn[:, :], length, ALU.mult, ALU.mult))
                assert steps[0] == V_X
                step(V.tensor_scalar(pk, yi, INV_2PI, MAGIC, ALU.mult, ALU.add))
                step(V.tensor_scalar(pk, pk, MAGIC, None, ALU.subtract))
                step(V.scalar_tensor_tensor(pf, pk, -TWO_PI_HI, yi, ALU.mult, ALU.add))
                step(V.scalar_tensor_tensor(pf, pk, -TWO_PI_LO, pf, ALU.mult, ALU.add))
                step(V.tensor_scalar(pf, pf, PI_SAFE, -PI_SAFE, ALU.min, ALU.max))
                assert steps[0] == V_F
                dve.wait_ge(pre_a, 4)
                step(V.tensor_scalar(dden, tau, -1.0, 1.0, ALU.mult, ALU.add))
                step(V.reciprocal(dden, dden))
                step(V.scalar_tensor_tensor(em, tau, 2.0, dden, ALU.mult, ALU.mult))
                step(V.tensor_tensor(hy, hy, hy, ALU.mult))
                step(V.tensor_scalar(t2, hy, -2.0, 1.0, ALU.mult, ALU.add))
                step(V.tensor_tensor(t2, em, t2, ALU.mult))
                step(V.scalar_tensor_tensor(nd_r, hy, -2.0, t2, ALU.mult, ALU.add))
                step(V.scalar_tensor_tensor(nd_i, em, 1.0, sy, ALU.add, ALU.mult))
                step(V.tensor_scalar(t0, nd_i[:, 1, :], lam_p[:, 1:2], None, ALU.mult))
                step(V.scalar_tensor_tensor(dr, nd_r[:, 1, :], lam_p[:, 0:1], t0, ALU.mult, ALU.subtract))
                step(V.tensor_scalar(t0, nd_i[:, 1, :], lam_p[:, 0:1], None, ALU.mult))
                step(V.scalar_tensor_tensor(di, nd_r[:, 1, :], lam_p[:, 1:2], t0, ALU.mult, ALU.add))
                step(V.tensor_tensor(q0, dr, dr, ALU.mult))
                step(V.tensor_tensor(q1, di, di, ALU.mult))
                step(V.scalar_tensor_tensor(q0, q0, RECIP_EPS, q1, ALU.add, ALU.add))
                step(V.reciprocal(q0, q0))
                step(V.tensor_tensor(t0, nd_r[:, 0, :], dr, ALU.mult))
                step(V.tensor_tensor(t1, nd_i[:, 0, :], di, ALU.mult))
                step(V.tensor_tensor(gr, t0, t1, ALU.add))
                step(V.tensor_tensor(gr, gr, q0, ALU.mult))
                step(V.tensor_tensor(t0, nd_i[:, 0, :], dr, ALU.mult))
                step(V.tensor_tensor(t1, nd_r[:, 0, :], di, ALU.mult))
                step(V.tensor_tensor(gi, t0, t1, ALU.subtract))
                step(V.tensor_tensor(gi, gi, q0, ALU.mult))
                step(V.tensor_scalar(t0, gi, odd, None, ALU.mult))
                step(V.scalar_tensor_tensor(rr[:, :], gr, even, t0, ALU.mult, ALU.subtract))
                step(V.tensor_scalar(t0, gr, odd, None, ALU.mult))
                step(V.scalar_tensor_tensor(ss[:, :], gi, neven, t0, ALU.mult, ALU.subtract))
                assert steps[0] == N_PRE

                def angles_a(k):
                    V.tensor_tensor(theta[:, :, :],
                                    zi[:, bass.ds(k * TC, TC)].unsqueeze(2).broadcast_to([P, TC, 2 * SEG]),
                                    pos[:, :].unsqueeze(1).broadcast_to([P, TC, 2 * SEG]),
                                    ALU.mult).then_inc(tab_v, 1)
                    dve.wait_ge(tab_v, TV * k + 1)
                    V.tensor_scalar(turns[:, :, :], theta[:, :, :], INV_2PI, MAGIC, ALU.mult, ALU.add).then_inc(tab_v, 1)
                    dve.wait_ge(tab_v, TV * k + 2)
                    V.tensor_scalar(turns[:, :, :], turns[:, :, :], MAGIC, None, ALU.subtract).then_inc(tab_v, 1)

                def angles_b(k):
                    dve.wait_ge(tab_v, TV * k + 3)
                    V.scalar_tensor_tensor(theta[:, :, :], turns[:, :, :], -TWO_PI_HI, theta[:, :, :],
                                           ALU.mult, ALU.add).then_inc(tab_v, 1)
                    dve.wait_ge(tab_v, TV * k + 4)
                    V.scalar_tensor_tensor(theta[:, :, :], turns[:, :, :], -TWO_PI_LO, theta[:, :, :],
                                           ALU.mult, ALU.add).then_inc(tab_v, 1)
                    dve.wait_ge(tab_v, TV * k + 5)
                    V.tensor_scalar(theta[:, :, :], theta[:, :, :], PI_SAFE, -PI_SAFE,
                                    ALU.min, ALU.max).then_inc(tab_v, 1)

                def table_r(k, ring, first):
                    dve.wait_ge(tab_a, TA * k + 4)
                    V.tensor_scalar(half[:, :, :], half[:, :, :], -2.0, 1.0, ALU.mult, ALU.add).then_inc(tab_v, 1)
                    dve.wait_ge(tab_v, TV * k + 7)
                    if not first:
                        dve.wait_ge(z_p, (k - 1) * PAIRS + 1)
                    V.tensor_tensor(tab_r[ring][:, :, :], expo[:, :, :], half[:, :, :], ALU.mult).then_inc(tab_v, 1)

                def digits_r(k, ring):
                    rr_b, ss_b = (a[:, bass.ds(k * TC, TC)].unsqueeze(2).broadcast_to([P, TC, SEG]) for a in (rr, ss))
                    dve.wait_ge(tab_v, TV * k + 8)
                    V.tensor_tensor(m1[:, :, :], rr_b, tab_r[ring][:, :, 0:SEG], ALU.mult).then_inc(tab_v, 1)
                    dve.wait_ge(tab_p, TP * k + 2)
                    V.tensor_tensor(m2[:, :, :], ss_b, tab_i[ring][:, :, 0:SEG], ALU.mult).then_inc(tab_v, 1)
                    dve.wait_ge(tab_v, TV * k + 10)
                    V.tensor_tensor(u_r[ring][:, :, :], m1[:, :, :], m2[:, :, :], ALU.add).then_inc(tab_v, 1)

                def summands(k, j, ring):
                    if j == 0:
                        dve.wait_ge(tab_v, TV * k + 11)
                        dve.wait_ge(tab_p, TP * k + 5)
                    dve.wait_ge(z_used, k * PAIRS + j + 1)
                    for s, n in ((0, 0), (0, 1), (1, 0)):
                        u, tab = ((u_r, tab_r), (u_i, tab_i))[n]
                        last = V.tensor_tensor(
                            z[j % 2][s][n][:, :].rearrange("p (a b) -> p a b", a=SEG),
                            u[ring][:, 2 * j + s, :].unsqueeze(2).broadcast_to([P, SEG, SEG]),
                            tab[ring][:, 2 * j + s, SEG:].unsqueeze(1).broadcast_to([P, SEG, SEG]),
                            ALU.mult)
                    last.then_inc(z_v, 1)

                def weight_lo(k, h, n):
                    ring = (3 * h + n) % 2
                    name, width = W_ITEMS[n]
                    dve.wait_ge(w_hi, 3 * k + n + 1)
                    hi, lo = (W[name + s][:, bass.ds(k, 1), :].rearrange("p k n -> p (k n)") for s in ("_hi", "_lo"))
                    V.scalar_tensor_tensor(lo, wst[ring][:, 0:width], WS, hi, ALU.mult, ALU.subtract).then_inc(w_lo, 1)

                def chunk(cc, h, last):
                    k = 2 * cc + h
                    for j in range(PAIRS):
                        summands(k, j, h)
                        if not last:
                            if j == 0:
                                angles_a(k + 1)
                            if j == 1:
                                angles_b(k + 1)
                            if j == 4:
                                table_r(k + 1, (h + 1) % 2, False)
                            if j == 6:
                                digits_r(k + 1, (h + 1) % 2)
                        if j in (3, 5, 7):
                            weight_lo(k, h, (j - 3) // 2)

                angles_a(0)
                angles_b(0)
                table_r(0, 0, True)
                digits_r(0, 0)
                with dve.Fori(0, CHUNKS // 2 - 1) as cc:
                    chunk(cc, 0, False)
                    chunk(cc, 1, False)
                chunk(CHUNKS // 2 - 1, 0, False)
                chunk(CHUNKS // 2 - 1, 1, True)
                for n in range(5):
                    dve.wait_ge(ffn_hi, n + 1)
                    hi, _ = ffn_parts(n, "hi")
                    lo, src = ffn_parts(n, "lo")
                    V.scalar_tensor_tensor(lo, src, WS, hi, ALU.mult, ALU.subtract).then_inc(ffn_lo, 1)

            @block.tensor
            def _(pe):
                pe.sem_inc(z_used, 2)

                def transposes(cc, h, half_):
                    k = 2 * cc + h
                    pe.wait_ge(x_in[h], 32 * cc + 32)
                    pe.wait_ge(xt_sb, 2 * k + half_ + 1)
                    for j in range(4):
                        last = pe.transpose(xps[half_][:, j * P:(j + 1) * P], xq[h][:, 4 * half_ + j, :], ident)
                    last.then_inc(xt_ps, 1)

                def pairs(cc, h, half_):
                    k = 2 * cc + h
                    pe.wait_ge(xt_sb, 2 * k + half_ + 3)
                    for j in range(4 * half_, 4 * half_ + 4):
                        pair = k * PAIRS + j
                        pe.wait_ge(z_v, pair + 2)
                        pe.wait_ge(z_p, pair + 2)
                        pe.wait_ge(h_copied, 2 * pair + 2)
                        for n in range(2):
                            for m in range(2):
                                for s in range(2):
                                    at = (j % 4) * P + 64 * s
                                    last = pe.matmul(hps[j % 2][n][64 * s:64 * s + 64, :], xt[half_][:, at:at + 64],
                                                     z[j % 2][s][m][:, n * 512:n * 512 + 512],
                                                     start=(m == 0), stop=(m == 1))
                        last.then_inc(z_used, 1)

                def chunk(cc, h, last):
                    transposes(cc, h, 1)
                    pairs(cc, h, 0)
                    if not last:
                        transposes(cc + h, (h + 1) % 2, 0)
                    pairs(cc, h, 1)

                pe.wait_ge(small_in, 80)
                transposes(0, 0, 0)
                with pe.Fori(0, CHUNKS // 2 - 1) as cc:
                    chunk(cc, 0, False)
                    chunk(cc, 1, False)
                chunk(CHUNKS // 2 - 1, 0, False)
                chunk(CHUNKS // 2 - 1, 1, True)
                pe.wait_ge(ffn_in, 16 * (2 + NF))
                for n in range(5):
                    if n >= 2:
                        pe.wait_ge(ffn_lo, n - 1 if n != 3 else 2)
                    if n == 4:
                        pe.wait_ge(ffn_lo, 3)
                    for k in range(KC if n == 2 else 4):
                        if n == 2:
                            last = pe.transpose(fps[0][:, k * NF:(k + 1) * NF], wr_st[0:NF, k * P:(k + 1) * P],
                                                ident[0:NF, 0:NF])
                        elif n < 2:
                            at = (4 * n + k) * P
                            last = pe.transpose(fps[n][:, k * P:(k + 1) * P], fa_st[:, at:at + P], ident)
                        else:
                            last = pe.transpose(fps[n % 2][:, k * P:(k + 1) * P], fb_st[:, 4 * (n - 3) + k, :], ident)
                    last.then_inc(ffn_t, 1)


V_X, V_F, N_PRE = 12, 17, 45



def layer_stage(nc, h0, out, W):
    with ExitStack() as ctx:
        def sb(name, shape, dt=f32):
            return ctx.enter_context(nc.sbuf_tensor(name, shape, dt))

        def sem(name):
            return ctx.enter_context(nc.semaphore(name))

        cst, ident16 = W["cst"], W["ident16"]
        ident = cst[:, C_IDENT:C_IDENT + P]
        mask = cst[:, C_MASK:C_MASK + P]

        h_ln = sb("h_ln", [P, D])
        h_res = sb("h_res", [P, D])
        xn = [sb(f"xn{i}", [P, D]) for i in range(2)]
        xt_hi = [sb(f"xt_hi{i}", [P, KC, P], f16) for i in range(2)]
        xt_lo = [sb(f"xt_lo{i}", [P, KC, P], f16) for i in range(2)]
        bn = [sb(f"bn{i}", [P, 12]) for i in range(2)]
        mv = [sb(f"mv{i}", [P, 2]) for i in range(2)]
        nrm = [sb(f"nrm{i}", [P, 8]) for i in range(2)]
        rt_c = sb("rt_c", [P, 512])
        rt_s = sb("rt_s", [P, 512])
        qr = sb("qr", [P, 512])
        qs = sb("qs", [P, H, 2, 2, HD], f16)
        kt_c = sb("kt_c", [P, G * HD])
        kt_s = sb("kt_s", [P, G * HD])
        kr = sb("kr", [P, G * HD])
        ks = sb("ks", [P, G, 2, 2, HD], f16)
        vf = sb("vf", [P, G * HD])
        v_hi = sb("v_hi", [P, G * HD], f16)
        v_lo = sb("v_lo", [P, G * HD], f16)
        qt = [sb(f"qt{i}", [P, HG * P], f16) for i in range(2)]
        kt = sb("kt", [P, G, P], f16)
        sm = [sb(f"sm{i}", [P, HG * P]) for i in range(2)]
        smin = [sb(f"smin{i}", [P, HG]) for i in range(2)]
        pr = [sb(f"pr{i}", [P, HG * P]) for i in range(2)]
        rsum = [sb(f"rsum{i}", [P, HG]) for i in range(2)]
        rinv = [sb(f"rinv{i}", [P, HG]) for i in range(2)]
        pt_hi = sb("pt_hi", [P, HG * P], f16)
        pt_lo = sb("pt_lo", [P, HG * P], f16)
        ctx_hi = sb("ctx_hi", [P, G, P], f16)
        ctx_lo = sb("ctx_lo", [P, G, P], f16)
        h1 = sb("h1", [P, D])
        z8 = sb("z8", [P, NF])
        e8 = sb("e8", [P, NF])
        w8 = sb("w8", [P, NF])
        s8 = sb("s8", [P, 4])
        ls = sb("ls", [P, P])
        ls_hi = sb("ls_hi", [P, P], f16)
        ls_lo = sb("ls_lo", [P, P], f16)
        h2 = sb("h2", [P, D])

        s_ps = [ctx.enter_context(nc.psum_tensor(f"s_ps{i}", [P, 512], f32)) for i in range(2)]
        pt_ps = ctx.enter_context(nc.psum_tensor("pt_ps", [P, 512], f32))
        pv_ps = ctx.enter_context(nc.psum_tensor("pv_ps", [P, 512], f32))
        pa = ctx.enter_context(nc.psum_tensor("pa", [P, 512], f32))
        pb = ctx.enter_context(nc.psum_tensor("pb", [P, 512], f32))
        tq = ctx.enter_context(nc.psum_tensor("tq", [P, 1024], f16))
        tx = ctx.enter_context(nc.psum_tensor("tx", [P, 512], f32))
        tx16 = tx[:, :].bitcast(f16)

        ln_in = sem("ln_in")
        res_in = sem("res_in")
        out_sent = sem("out_sent")
        s_done = sem("s_done")
        qt_done = sem("qt_done")
        pt_done = sem("pt_done")
        pv_done = sem("pv_done")
        kv_done = sem("kv_done")
        q_done = sem("q_done")
        wo_done = sem("wo_done")
        ctx_used = sem("ctx_used")
        low_done = sem("low_done")
        out_done = sem("out_done")
        xt_done = [sem(f"xt_done{i}") for i in range(2)]
        kt_done = sem("kt_done")
        lst_done = sem("lst_done")
        qt_copied = sem("qt_copied")
        kt_copied = sem("kt_copied")
        exp_done = sem("exp_done")
        pth_done = sem("pth_done")
        ctxh_done = sem("ctxh_done")
        ln_y = [sem(f"ln_y{i}") for i in range(2)]
        ln_x = [sem(f"ln_x{i}") for i in range(2)]
        xth_done = [sem(f"xth_done{i}") for i in range(2)]
        low_e = sem("low_e")
        lsh_done = sem("lsh_done")
        qh_done = sem("qh_done")
        kh_done = sem("kh_done")
        vh_done = sem("vh_done")
        waits_held = sem("waits_held")
        masked = sem("masked")
        rinv_done = sem("rinv_done")
        ptl_done = sem("ptl_done")
        ctxl_done = sem("ctxl_done")
        ln_v = [sem(f"ln_v{i}") for i in range(2)]
        xtl_done = [sem(f"xtl_done{i}") for i in range(2)]
        kv_used = sem("kv_used")
        q_used = sem("q_used")
        h1_done = sem("h1_done")
        h2_done = sem("h2_done")
        low_v = sem("low_v")
        lsl_done = sem("lsl_done")
        qd_done = sem("qd_done")
        kd_done = sem("kd_done")
        q_sum = sem("q_sum")
        ql_done = sem("ql_done")
        k_sum = sem("k_sum")
        kl_done = sem("kl_done")
        vl_done = sem("vl_done")
        p_norm = sem("p_norm")

        FIRST, LAST = 3, NB - 3

        def has(b):
            return not isinstance(b, int) or 0 <= b < NB

        def reached(eng, s, per, b, k=0):
            if isinstance(b, int):
                if b < 0 or per * b + k == 0:
                    return
                if b >= NB:
                    b, k = NB, 0
            eng.wait_ge(s, per * b + k)

        def hold_waits(dve):
            dve.sem_inc(waits_held, 1)

        def group(i, s):
            return (i - 1, s + G) if s < 0 else (i + 1, s - G) if s >= G else (i, s)

        def bank_free(pe, i, tiles, n):
            for m, (s, per, ahead, k) in enumerate(tiles):
                if isinstance(i, int) or m == (n - 1) % len(tiles):
                    reached(pe, s, per, i + ahead - (m >= n), k)

        def wo_free(eng, b, g):
            if g < KC - 1:
                reached(eng, ctx_used, KC - 1, b - 1, g + 1)
            else:
                reached(eng, wo_done, 2, b)

        PA = ((kv_used, 1, 1, 1), (h2_done, 2, -2, 2), (h1_done, 2, -1, 2), (q_used, 2, 1, 2))
        PB = ((h2_done, 2, -2, 1), (h1_done, 2, -1, 1), (q_used, 2, 1, 1), (low_v, 5, -1, 5))
        TX = ((xtl_done[0], 2, 1, 2), (lsl_done, 1, -2, 1), (kt_copied, 2, 1, 1), (xtl_done[1], 2, -1, 1),
              (xtl_done[1], 2, -1, 2), (kt_copied, 2, 1, 2), (xtl_done[0], 2, 2, 1))

        def bodies(eng, body):
            for i in range(-2, FIRST):
                body(i)
            with eng.Fori(FIRST, LAST) as i:
                body(i)
            for i in range(LAST, NB + 2):
                body(i)

        with nc.Block() as block:
            @block.sync
            def _(sp):
                def row(ap, b):
                    return ap[bass.ds(b, 1), :, :].rearrange("b t d -> (b t) d")

                def body(i):
                    if has(i - 1):
                        reached(sp, h1_done, 2, i - 1)
                        sp.dma_start(h_res[:, :], row(h0, i - 1)).then_inc(res_in, 16)
                    if has(i - 2):
                        reached(sp, h2_done, 2, i - 2, 2)
                        sp.dma_start(row(out, i - 2), h2[:, :]).then_inc(out_sent, 16)
                    if has(i + 3):
                        reached(sp, ln_x[0], 1, i + 2, 1)
                        sp.dma_start(h_ln[:, :], row(h0, i + 3)).then_inc(ln_in, 16)

                sp.dma_start(h_ln[:, :], row(h0, 0)).then_inc(ln_in, 16)
                bodies(sp, body)
                sp.wait_ge(out_sent, 16 * NB)

            @block.tensor
            def _(pe):
                def products(ps, x_hi, x_lo, name, cols, k0, k1):
                    w_hi, w_lo = W[name + "_hi"], W[name + "_lo"]
                    for k in range(k0, k1):
                        pe.matmul(ps, x_hi[:, k, :], w_hi[:, k, cols], start=(k == 0), stop=False)
                        pe.matmul(ps, x_hi[:, k, :], w_lo[:, k, cols], start=False, stop=False)
                        last = pe.matmul(ps, x_lo[:, k, :], w_hi[:, k, cols], start=False, stop=(k == KC - 1))
                    return last

                def scores(i, s):
                    if not has(i):
                        return
                    reached(pe, qt_copied, G, i, s + 1)
                    if s == 0 or s == G // 2:
                        reached(pe, kt_copied, 2, i, 1 + s // (G // 2))
                    b, g = group(i, s - 2)
                    reached(pe, masked, 4 * G, b, 4 * (g + 1))
                    for j in range(HG):
                        last = pe.matmul(s_ps[s % 2][:, j * P:(j + 1) * P], qt[s % 2][:, j * P:(j + 1) * P],
                                         kt[:, s, :], start=True, stop=True)
                    last.then_inc(s_done, 1)

                def q_transpose(b, g):
                    if not has(b):
                        return
                    reached(pe, qd_done, 2, b, 1 + g // (G // 2))
                    reached(pe, qt_copied, G, b, g)
                    for j in range(HG):
                        last = pe.transpose(tq[:, j * P:(j + 1) * P],
                                            qs[:, HG * g + j, :, :, :].rearrange("p a b d -> p (a b d)"),
                                            ident16[:, :])
                    last.then_inc(qt_done, 1)

                def p_transpose(b, g):
                    if not has(b):
                        return
                    reached(pe, p_norm, G, b, g + 1)
                    reached(pe, ptl_done, G, b, g)
                    for j in range(HG):
                        last = pe.transpose(pt_ps[:, j * P:(j + 1) * P], pr[g % 2][:, j * P:(j + 1) * P], ident)
                    last.then_inc(pt_done, 1)

                def values(b, g):
                    if not has(b):
                        return
                    reached(pe, ptl_done, G, b, g + 1)
                    reached(pe, vl_done, 1, b, 1)
                    reached(pe, ctxl_done, G, b, g)
                    for n, (v, pt) in enumerate(((v_hi, pt_hi), (v_lo, pt_hi), (v_hi, pt_lo))):
                        for j in range(HG):
                            last = pe.matmul(pv_ps[j * HD:(j + 1) * HD, 0:P], v[:, g * HD:(g + 1) * HD],
                                             pt[:, j * P:(j + 1) * P], start=(n == 0), stop=(n == 2))
                    last.then_inc(pv_done, 1)

                def x_transpose(w, b, tile, i, n):
                    if not has(b):
                        return
                    reached(pe, ln_x[w], 1, b, 1)
                    bank_free(pe, i, TX, n)
                    for j in range(4):
                        at = (4 * tile + j) * P
                        last = pe.transpose(tx[:, j * P:(j + 1) * P], xn[w][:, at:at + P], ident)
                    last.then_inc(xt_done[w], 1)

                def k_transpose(b, tile, i, n):
                    if not has(b):
                        return
                    reached(pe, kd_done, 1, b, 1)
                    bank_free(pe, i, TX, n)
                    for j in range(4):
                        last = pe.transpose(tx16[:, j * P:(j + 1) * P],
                                            ks[:, 4 * tile + j, :, :, :].rearrange("p a b d -> p (a b d)"),
                                            ident16[:, :])
                    last.then_inc(kt_done, 1)

                def kv(i, k0, k1):
                    if not has(i + 1):
                        return
                    if k0 == 0:
                        bank_free(pe, i, PA, 0)
                    reached(pe, xtl_done[0], 2, i + 1, 1 + (k1 > 4))
                    last = products(pa[:, :], xt_hi[0], xt_lo[0], "wkv", slice(0, 512), k0, k1)
                    if k1 == KC:
                        last.then_inc(kv_done, 1)

                def q_half(i, half, k0, k1):
                    if not has(i + 1):
                        return
                    if k0 == 0:
                        bank_free(pe, i, (PB, PA)[half], (2, 3)[half])
                    last = products((pb, pa)[half][:, :], xt_hi[0], xt_lo[0], "wq",
                                    slice(512 * half, 512 * half + 512), k0, k1)
                    if k1 == KC:
                        last.then_inc(q_done, 1)

                def out_half(i, half):
                    if not has(i - 2):
                        return
                    reached(pe, lsl_done, 1, i - 2, 1)
                    bank_free(pe, i, (PB, PA)[half], (0, 1)[half])
                    ps, cols = (pb, pa)[half], slice(512 * half, 512 * half + 512)
                    pe.matmul(ps[:, :], ls_hi[:, :], W["bm_hi"][:, cols], start=True, stop=False)
                    pe.matmul(ps[:, :], ls_hi[:, :], W["bm_lo"][:, cols], start=False, stop=False)
                    pe.matmul(ps[:, :], ls_lo[:, :], W["bm_hi"][:, cols], start=False, stop=True).then_inc(out_done, 1)

                def wo_half(i, half, k0, k1):
                    if not has(i - 1):
                        return
                    if k0 == 0:
                        bank_free(pe, i, (PB, PA)[half], (1, 2)[half])
                    for k in range(k0, k1):
                        if half == 0:
                            reached(pe, ctxl_done, G, i - 1, k + 1)
                        last = products((pb, pa)[half][:, :], ctx_hi, ctx_lo, "wo",
                                        slice(512 * half, 512 * half + 512), k, k + 1)
                        if half == 1 and k < KC - 1:
                            last.then_inc(ctx_used, 1)
                    if k1 == KC:
                        last.then_inc(wo_done, 1)

                def low(i):
                    if not has(i - 1):
                        return
                    bank_free(pe, i, PB, 3)
                    reached(pe, xtl_done[1], 2, i - 1, 2)
                    products(pb[:, 0:AW], xt_hi[1], xt_lo[1], "aw", slice(0, AW), 0, KC).then_inc(low_done, 1)

                def ls_transpose(i):
                    if not has(i - 2):
                        return
                    reached(pe, low_v, 5, i - 2, 5)
                    bank_free(pe, i, TX, 1)
                    pe.transpose(tx[:, 0:P], ls[:, :], ident).then_inc(lst_done, 1)

                def body(i):
                    for s in range(G):
                        scores(i, s)
                        q_transpose(*group(i, s + 1))
                        values(*group(i, s - 2))
                        if s == 0:
                            x_transpose(0, i + 1, 1, i, 0)
                            kv(i, 0, 3)
                        if s == 1:
                            ls_transpose(i)
                            kv(i, 6, 8)
                        if s == 2:
                            wo_half(i, 0, 0, 3)
                        if s == 3:
                            wo_half(i, 0, 3, 6)
                        if s == 4:
                            wo_half(i, 0, 6, 8)
                            wo_half(i, 1, 6, 7)
                        if s == 5:
                            q_half(i, 0, 3, 6)
                        if s == 6:
                            q_half(i, 1, 1, 4)
                        if s == 7:
                            x_transpose(1, i - 1, 1, i, 4)
                            q_half(i, 1, 7, 8)
                        p_transpose(*group(i, s - 1))
                        if s == 0:
                            kv(i, 3, 6)
                        if s == 1:
                            out_half(i, 0)
                            out_half(i, 1)
                        if s == 2:
                            wo_half(i, 1, 0, 3)
                        if s == 3:
                            wo_half(i, 1, 3, 6)
                        if s == 4:
                            wo_half(i, 1, 7, 8)
                            k_transpose(i + 1, 0, i, 2)
                            q_half(i, 0, 0, 3)
                        if s == 5:
                            q_half(i, 0, 6, 8)
                            q_half(i, 1, 0, 1)
                        if s == 6:
                            x_transpose(1, i - 1, 0, i, 3)
                            q_half(i, 1, 4, 7)
                        if s == 7:
                            k_transpose(i + 1, 1, i, 5)
                            low(i)
                            x_transpose(0, i + 2, 0, i, 6)

                bodies(pe, body)

            @block.scalar
            def _(act):
                A = nc.scalar

                def copy_qt(b, g):
                    if not has(b):
                        return
                    reached(act, qt_done, G, b, g + 1)
                    pb_, pg = group(b, g - 2)
                    reached(act, s_done, G, pb_, pg + 1)
                    A.activation(qt[g % 2][:, :], tq[:, 0:HG * P], ACT.Copy).then_inc(qt_copied, 1)

                def exps(b, g):
                    if not has(b):
                        return
                    pb_, pg = group(b, g - 2)
                    reached(act, pt_done, G, pb_, pg + 1)
                    for j in range(HG):
                        reached(act, masked, 4 * G, b, 4 * g + j + 1)
                        last = A.activation(pr[g % 2][:, j * P:(j + 1) * P], sm[g % 2][:, j * P:(j + 1) * P], ACT.Exp,
                                            bias=smin[g % 2][:, j:j + 1], scale=-1.0,
                                            accum_out=rsum[g % 2][:, j:j + 1])
                    last.then_inc(exp_done, 1)

                def pt_high(b, g):
                    if not has(b):
                        return
                    reached(act, pt_done, G, b, g + 1)
                    A.activation(pt_hi[:, :], pt_ps[:, :], ACT.Copy).then_inc(pth_done, 1)

                def ctx_high(b, g):
                    if not has(b):
                        return
                    reached(act, pv_done, G, b, g + 1)
                    wo_free(act, b, g)
                    A.activation(ctx_hi[:, g, :], pv_ps[:, 0:P], ACT.Copy).then_inc(ctxh_done, 1)

                def norm_root(w, b):
                    if not has(b):
                        return
                    reached(act, ln_v[w], 8, b, 4)
                    A.activation(nrm[w][:, 1:2], nrm[w][:, 0:1], ACT.Ln).then_inc(ln_y[w], 1)
                    reached(act, ln_y[w], 2, b, 1)
                    A.activation(nrm[w][:, 2:3], nrm[w][:, 1:2], ACT.Exp, scale=-0.5).then_inc(ln_y[w], 1)

                def norm_apply(w, b):
                    if not has(b):
                        return
                    reached(act, ln_v[w], 8, b, 8)
                    reached(act, xt_done[w], 2, b)
                    A.activation(xn[w][:, :], (h_ln, h1)[w][:, :], ACT.Identity, bias=nrm[w][:, 6:7],
                                 scale=nrm[w][:, 5:6]).then_inc(ln_x[w], 1)

                def xt_high(w, b, tile):
                    if not has(b):
                        return
                    reached(act, xt_done[w], 2, b, tile + 1)
                    A.activation(xt_hi[w][:, 4 * tile:4 * tile + 4, :],
                                 tx[:, :].rearrange("p (k t) -> p k t", k=4), ACT.Copy).then_inc(xth_done[w], 1)

                def copy_kt(b, tile):
                    if not has(b):
                        return
                    reached(act, kt_done, 2, b, tile + 1)
                    A.activation(kt[:, 4 * tile:4 * tile + 4, :],
                                 tx16[:, 0:4 * P].rearrange("p (k t) -> p k t", k=4), ACT.Copy).then_inc(kt_copied, 1)

                def q_high(b, half):
                    if not has(b):
                        return
                    reached(act, q_sum, 2, b, half + 1)
                    reached(act, qt_done, G, b - 1, 4 * half + 4)
                    A.activation(qs[:, 16 * half:16 * half + 16, 0, 0, :],
                                 qr[:, :].rearrange("p (h d) -> p h d", d=HD), ACT.Copy).then_inc(qh_done, 1)

                def k_high(b):
                    if not has(b):
                        return
                    reached(act, k_sum, 1, b, 1)
                    reached(act, kt_done, 2, b)
                    A.activation(ks[:, :, 0, 0, :], kr[:, :].rearrange("p (h d) -> p h d", d=HD),
                                 ACT.Copy).then_inc(kh_done, 1)

                def v_high(b):
                    if not has(b):
                        return
                    reached(act, kv_used, 1, b, 1)
                    reached(act, pv_done, G, b)
                    A.activation(v_hi[:, :], vf[:, :], ACT.Copy).then_inc(vh_done, 1)

                def router_exp(b):
                    if not has(b):
                        return
                    reached(act, low_v, 5, b, 2)
                    A.activation(e8[:, :], z8[:, :], ACT.Exp, bias=s8[:, 0:1],
                                 accum_out=s8[:, 1:2]).then_inc(low_e, 1)

                def ls_high(b):
                    if not has(b):
                        return
                    reached(act, lst_done, 1, b, 1)
                    reached(act, out_done, 2, b)
                    A.activation(ls_hi[:, :], tx[:, 0:P], ACT.Copy).then_inc(lsh_done, 1)

                def body(i):
                    for s in range(G):
                        copy_qt(*group(i, s + 1))
                        if s == 0:
                            router_exp(i - 2)
                            xt_high(0, i + 1, 1)
                        if s == 1:
                            ls_high(i - 2)
                            v_high(i)
                        if s == 6:
                            norm_apply(1, i - 1)
                        if s == 7:
                            xt_high(1, i - 1, 1)
                        exps(i, s)
                        if s == 0:
                            q_high(i, 1)
                        if s == 3:
                            k_high(i + 1)
                        ctx_high(*group(i, s - 2))
                        pt_high(*group(i, s - 1))
                        if s == 2:
                            norm_root(0, i + 2)
                        if s == 4:
                            norm_apply(0, i + 2)
                            copy_kt(i + 1, 0)
                        if s == 5:
                            norm_root(1, i - 1)
                        if s == 6:
                            q_high(i + 1, 0)
                            xt_high(1, i - 1, 0)
                        if s == 7:
                            copy_kt(i + 1, 1)
                            xt_high(0, i + 2, 0)

                A.preload_act_table_set("natural_log_exp_and_others")
                bodies(act, body)

            @block.vector
            def _(dve):
                V = nc.vector

                def mask_min(b, g):
                    if not has(b):
                        return
                    reached(dve, s_done, G, b, g + 1)
                    pb_, pg = group(b, g - 2)
                    reached(dve, exp_done, G, pb_, pg + 1)
                    hold_waits(dve)
                    for j in range(HG):
                        V.tensor_tensor_reduce(sm[g % 2][:, j * P:(j + 1) * P], s_ps[g % 2][:, j * P:(j + 1) * P],
                                               mask, 1.0, 3e38, ALU.add, ALU.min,
                                               smin[g % 2][:, j:j + 1]).then_inc(masked, 1)

                def reciprocals(b, g):
                    if not has(b):
                        return
                    reached(dve, exp_done, G, b, g + 1)
                    V.reciprocal(rinv[g % 2][:, :], rsum[g % 2][:, :]).then_inc(rinv_done, 1)

                def pt_low(b, g):
                    if not has(b):
                        return
                    reached(dve, pth_done, G, b, g + 1)
                    V.tensor_tensor(pt_lo[:, :], pt_ps[:, :], pt_hi[:, :], ALU.subtract).then_inc(ptl_done, 1)

                def ctx_low(b, g):
                    if not has(b):
                        return
                    reached(dve, ctxh_done, G, b, g + 1)
                    V.tensor_tensor(ctx_lo[:, g, :], pv_ps[:, 0:P], ctx_hi[:, g, :], ALU.subtract).then_inc(ctxl_done, 1)

                def norm_half(w, src, b, half):
                    V.bn_stats(bn[w][:, 6 * half:6 * half + 6], src[:, 512 * half:512 * half + 512]).then_inc(ln_v[w], 1)

                def norm_stats(w, b):
                    reached(dve, ln_v[w], 8, b, 2)
                    hold_waits(dve)
                    V.bn_aggr(mv[w][:, :], bn[w][:, :]).then_inc(ln_v[w], 1)
                    reached(dve, ln_v[w], 8, b, 3)
                    V.tensor_scalar(nrm[w][:, 0:1], mv[w][:, 1:2], LN_EPS, None, ALU.add).then_inc(ln_v[w], 1)

                def norm_refine(w, b):
                    if not has(b):
                        return
                    v, y, a, c, scale, shift = (nrm[w][:, n:n + 1] for n in (0, 2, 3, 4, 5, 6))
                    reached(dve, ln_y[w], 2, b, 2)
                    V.scalar_tensor_tensor(a, y, v, y, ALU.mult, ALU.mult).then_inc(ln_v[w], 1)
                    reached(dve, ln_v[w], 8, b, 5)
                    V.tensor_scalar(c, a, -0.5, 1.5, ALU.mult, ALU.add).then_inc(ln_v[w], 1)
                    reached(dve, ln_v[w], 8, b, 6)
                    V.tensor_tensor(scale, y, c, ALU.mult).then_inc(ln_v[w], 1)
                    reached(dve, ln_v[w], 8, b, 7)
                    V.scalar_tensor_tensor(shift, mv[w][:, 0:1], -1.0, scale, ALU.mult, ALU.mult).then_inc(ln_v[w], 1)

                def norm1_stats(b):
                    if not has(b):
                        return
                    dve.wait_ge(ln_in, 16 * b + 16)
                    norm_half(0, h_ln, b, 0)
                    norm_half(0, h_ln, b, 1)
                    norm_stats(0, b)

                def xt_low(w, b, tile):
                    if not has(b):
                        return
                    reached(dve, xth_done[w], 2, b, tile + 1)
                    V.tensor_tensor(xt_lo[w][:, 4 * tile:4 * tile + 4, :], tx[:, :].rearrange("p (k t) -> p k t", k=4),
                                    xt_hi[w][:, 4 * tile:4 * tile + 4, :], ALU.subtract).then_inc(xtl_done[w], 1)

                def rotate(cos_part, sin_part, src, n, at_c, at_s):
                    x4 = src.rearrange("p (h a d) -> p h a d", h=n, a=2)
                    c = cst[:, at_c:at_c + HD].unsqueeze(1).broadcast_to([P, n, HD])
                    V.tensor_tensor(cos_part.rearrange("p (h d) -> p h d", d=HD),
                                    src.rearrange("p (h d) -> p h d", d=HD), c, ALU.mult)
                    y4 = sin_part.rearrange("p (h a d) -> p h a d", h=n, a=2)
                    for a in range(2):
                        sn = cst[:, at_s + a * HD // 2:at_s + (a + 1) * HD // 2]
                        last = V.tensor_tensor(y4[:, :, a, :], x4[:, :, 1 - a, :],
                                               sn.unsqueeze(1).broadcast_to([P, n, HD // 2]), ALU.mult)
                    return last

                def kv_rotate(b):
                    if not has(b):
                        return
                    reached(dve, kv_done, 1, b, 1)
                    reached(dve, vl_done, 1, b)
                    reached(dve, k_sum, 1, b)
                    V.tensor_scalar(vf[:, :], pa[:, G * HD:], INV_WS, None, ALU.mult)
                    rotate(kt_c[:, :], kt_s[:, :], pa[:, 0:G * HD], G, C_KC, C_KS).then_inc(kv_used, 1)

                def q_rotate(b, half):
                    if not has(b):
                        return
                    reached(dve, q_done, 2, b, half + 1)
                    reached(dve, q_sum, 2, b, half)
                    rotate(rt_c[:, :], rt_s[:, :], (pb, pa)[half][:, :], H // 2, C_QC, C_QS).then_inc(q_used, 1)

                def q_double(b, half):
                    if not has(b):
                        return
                    reached(dve, qh_done, 2, b, half + 1)
                    reached(dve, ql_done, 2, b, half + 1)
                    part = qs[:, 16 * half:16 * half + 16, :, :, :].rearrange("p h a b d -> p h a (b d)")
                    V.tensor_copy(part[:, :, 1, :], part[:, :, 0, :]).then_inc(qd_done, 1)

                def k_double(b):
                    if not has(b):
                        return
                    reached(dve, kh_done, 1, b, 1)
                    reached(dve, kl_done, 1, b, 1)
                    part = ks[:, :, :, :, :].rearrange("p g a b d -> p (g a) b d")
                    V.tensor_copy(part[:, :, 1, :], part[:, :, 0, :]).then_inc(kd_done, 1)

                def residual1(b, half):
                    if not has(b):
                        return
                    reached(dve, wo_done, 2, b, half + 1)
                    dve.wait_ge(res_in, 16 * b + 16)
                    cols = slice(512 * half, 512 * half + 512)
                    V.scalar_tensor_tensor(h1[:, cols], (pb, pa)[half][:, :], INV_WS, h_res[:, cols],
                                           ALU.mult, ALU.add).then_inc(h1_done, 1)
                    reached(dve, h1_done, 2, b, half + 1)
                    norm_half(1, h1, b, half)
                    if half == 1:
                        norm_stats(1, b)

                def residual2(b, half):
                    if not has(b):
                        return
                    reached(dve, out_done, 2, b, half + 1)
                    if half == 0:
                        reached(dve, out_sent, 16, b)
                    cols = slice(512 * half, 512 * half + 512)
                    V.scalar_tensor_tensor(h2[:, cols], (pb, pa)[half][:, :], INV_WS, h1[:, cols],
                                           ALU.mult, ALU.add).then_inc(h2_done, 1)

                def router_max(b):
                    if not has(b):
                        return
                    reached(dve, low_done, 1, b, 1)
                    V.scalar_tensor_tensor(z8[:, :], pb[:, P:AW], INV_WS, W["br_all"][:, :],
                                           ALU.mult, ALU.add).then_inc(low_v, 1)
                    reached(dve, low_v, 5, b, 1)
                    V.tensor_reduce(s8[:, 0:1], z8[:, :], AX.X, ALU.max, negate=True).then_inc(low_v, 1)

                def router_weights(b):
                    if not has(b):
                        return
                    reached(dve, low_e, 1, b, 1)
                    V.reciprocal(s8[:, 2:3], s8[:, 1:2]).then_inc(low_v, 1)
                    reached(dve, low_v, 5, b, 3)
                    V.tensor_scalar(w8[:, :], e8[:, :], s8[:, 2:3], FFN_SCALE * INV_WS, ALU.mult, ALU.mult).then_inc(low_v, 1)
                    reached(dve, low_v, 5, b, 4)
                    V.tensor_tensor(ls[:, :].rearrange("p (h r) -> p h r", r=R),
                                    pb[:, 0:P].rearrange("p (h r) -> p h r", r=R),
                                    w8[:, :].unsqueeze(2).broadcast_to([P, NF, R]), ALU.mult).then_inc(low_v, 1)

                def ls_low(b):
                    if not has(b):
                        return
                    reached(dve, lsh_done, 1, b, 1)
                    V.tensor_tensor(ls_lo[:, :], tx[:, 0:P], ls_hi[:, :], ALU.subtract).then_inc(lsl_done, 1)

                def body(i):
                    for s in range(G):
                        mask_min(i, s)
                        if s == 0:
                            router_max(i - 2)
                            xt_low(0, i + 1, 1)
                            router_weights(i - 2)
                        if s == 1:
                            ls_low(i - 2)
                            kv_rotate(i + 1)
                        if s == 3:
                            norm_refine(0, i + 2)
                        if s == 6:
                            pass
                        if s == 7:
                            xt_low(1, i - 1, 1)
                        reciprocals(i, s)
                        if s == 1:
                            q_double(i, 1)
                        ctx_low(*group(i, s - 2))
                        pt_low(*group(i, s - 1))
                        if s == 1:
                            residual2(i - 2, 0)
                            residual2(i - 2, 1)
                        if s == 2:
                            norm1_stats(i + 2)
                        if s == 3:
                            k_double(i + 1)
                        if s == 4:
                            residual1(i - 1, 0)
                            residual1(i - 1, 1)
                        if s == 5:
                            norm_refine(1, i - 1)
                            q_rotate(i + 1, 0)
                        if s == 6:
                            q_double(i + 1, 0)
                            xt_low(1, i - 1, 0)
                        if s == 7:
                            q_rotate(i + 1, 1)
                            xt_low(0, i + 2, 0)

                bodies(dve, body)

            @block.gpsimd
            def _(pool):
                def normalise(b, g):
                    if not has(b):
                        return
                    reached(pool, rinv_done, G, b, g + 1)
                    p3 = pr[g % 2][:, :].rearrange("p (j k) -> p j k", j=HG)
                    nc.gpsimd.tensor_tensor(p3, p3, rinv[g % 2][:, :].unsqueeze(2).broadcast_to([P, HG, P]),
                                            ALU.mult).then_inc(p_norm, 1)

                def sum_q(b, half):
                    if not has(b):
                        return
                    reached(pool, q_used, 2, b, half + 1)
                    pb_, ph = (b, 0) if half else (b - 1, 1)
                    reached(pool, qh_done, 2, pb_, ph + 1)
                    reached(pool, ql_done, 2, pb_, ph + 1)
                    nc.gpsimd.tensor_tensor(qr[:, :], rt_c[:, :], rt_s[:, :], ALU.add).then_inc(q_sum, 1)

                def q_low(b, half):
                    if not has(b):
                        return
                    reached(pool, qh_done, 2, b, half + 1)
                    part = qs[:, 16 * half:16 * half + 16, 0, :, :]
                    nc.gpsimd.tensor_tensor(part[:, :, 1, :], qr[:, :].rearrange("p (h d) -> p h d", d=HD),
                                            part[:, :, 0, :], ALU.subtract).then_inc(ql_done, 1)

                def sum_k(b):
                    if not has(b):
                        return
                    reached(pool, kv_used, 1, b, 1)
                    reached(pool, kh_done, 1, b)
                    reached(pool, kl_done, 1, b)
                    nc.gpsimd.tensor_tensor(kr[:, :], kt_c[:, :], kt_s[:, :], ALU.add).then_inc(k_sum, 1)

                def k_low(b):
                    if not has(b):
                        return
                    reached(pool, kh_done, 1, b, 1)
                    nc.gpsimd.tensor_tensor(ks[:, :, 1, 0, :], kr[:, :].rearrange("p (h d) -> p h d", d=HD),
                                            ks[:, :, 0, 0, :], ALU.subtract).then_inc(kl_done, 1)

                def v_low(b):
                    if not has(b):
                        return
                    reached(pool, vh_done, 1, b, 1)
                    nc.gpsimd.tensor_tensor(v_lo[:, :], vf[:, :], v_hi[:, :], ALU.subtract).then_inc(vl_done, 1)

                def body(i):
                    for s in range(G):
                        if s == 0:
                            sum_q(i, 1)
                        if s == 1:
                            v_low(i)
                        normalise(i, s)
                        if s == 0:
                            q_low(i, 1)
                        if s == 2:
                            sum_k(i + 1)
                        if s == 3:
                            k_low(i + 1)
                        if s == 6:
                            sum_q(i + 1, 0)
                            q_low(i + 1, 0)

                bodies(pool, body)


_INS = ['x', 'L0_tok_log_dt', 'L0_tok_Lambda', 'L0_attn_Wq', 'L0_attn_Wk', 'L0_attn_Wv', 'L0_attn_Wo',
        'L0_ffn_A', 'L0_ffn_B', 'L0_ffn_Wr', 'L0_ffn_br']


def kernel(**inputs):
    import concourse.bacc as bacc
    from concourse.bass_utils import run_bass_kernel_spmd

    nc = bacc.Bacc("TRN2", target_bir_lowering=False, num_devices=1)
    arrays, args = {}, []
    for name in _INS:
        arrays[name] = np.ascontiguousarray(inputs[name])
        args.append(nc.dram_tensor(name, arrays[name].shape, f32, kind="ExternalInput").ap())
    arrays["consts"] = constants()
    args.append(nc.dram_tensor("consts", (P, C_N), f32, kind="ExternalInput").ap())
    h0 = nc.dram_tensor("h0", (NB, T, D), f32).ap()
    out = nc.dram_tensor("out", (NB, T, D), f32, kind="ExternalOutput").ap()
    x, log_dt, lam, wq, wk, wv, wo, fa, fb, wr, br, consts = args
    vit_layer(nc, x, log_dt, lam, wq, wk, wv, wo, fa, fb, wr, br, consts, h0, out)
    r = run_bass_kernel_spmd(nc, [arrays], core_ids=[0])
    return r.results[0]["out"]
```

```python
from contextlib import ExitStack

import concourse.bass as bass
import numpy as np
from concourse import mybir

f32 = mybir.dt.float32
f16 = mybir.dt.float16
ALU = mybir.AluOpType
ACT = mybir.ActivationFunctionType
AX = mybir.AxisListType

P = 128
NB = 64
T = 128
D = 1024
NS = 64
H, G, HD = 32, 8, 32
HG = H // G
KC = D // P
NF, R = 8, 16
AW = NF * R + NF
WS = 64.0
INV_WS = 1.0 / WS
LN_EPS = 1e-5
RECIP_EPS = 1e-7
SEG = 32
HALF = D // 2
DIG = HALF // SEG
NPOS = DIG + SEG
FFN_SCALE = 2.0 * NF
ROPE_BASE = 500000.0

TC = 16
CHUNKS = T // TC
PAIRS = TC // 2
QUAD = PAIRS // 2
ZR = 4
SUMMED = (2, 3, 7)
MAGIC = 12582912.0
INV_2PI = 0.15915494309189535
TWO_PI_HI = 6.28125
TWO_PI_LO = 2.0 * float(np.pi) - 6.28125
PI_SAFE = 3.1415925

C_IDENT, C_MASK = 0, 128
C_QC, C_QS, C_KC, C_KS = 256, 288, 320, 352
C_POS, C_END, C_RE, C_IM, C_NRE, C_SIGN = 384, 432, 434, 435, 436, 437
C_N = 438


def constants():
    c = np.zeros((P, C_N), np.float32)
    c[:, C_IDENT:C_IDENT + P] = np.eye(P, dtype=np.float32)
    c[:, C_MASK:C_MASK + P] = np.triu(np.full((P, P), 1e30, np.float32), k=1)
    inv_freq = (1.0 / np.float32(ROPE_BASE) ** (np.arange(0, HD, 2, dtype=np.float32) / HD)).astype(np.float32)
    freqs = np.arange(T, dtype=np.float32)[:, None] * inv_freq[None]
    cos, sin = np.cos(freqs).astype(np.float64), np.sin(freqs).astype(np.float64)
    for at_c, at_s, s in ((C_QC, C_QS, -INV_WS / np.sqrt(HD)), (C_KC, C_KS, INV_WS)):
        c[:, at_c:at_c + HD] = np.concatenate([cos, cos], 1) * s
        c[:, at_s:at_s + HD] = np.concatenate([-sin, sin], 1) * s
    c[:, C_POS:C_POS + DIG] = np.arange(0, HALF, SEG)
    c[:, C_POS + DIG:C_POS + NPOS] = np.arange(SEG)
    c[:, C_END] = -(HALF - SEG)
    c[:, C_END + 1] = -(SEG - 1)
    c[:NS, C_RE] = 1.0
    c[NS:, C_IM] = 1.0
    c[:NS, C_NRE] = -1.0
    c[:NS, C_SIGN] = -1.0
    c[NS:, C_SIGN] = 1.0
    return c


def vit_layer(nc, x, log_dt, lam, wq, wk, wv, wo, fa, fb, wr, br, consts, h0, out):
    with ExitStack() as keep:
        def sbk(name, shape, dt=f32):
            return keep.enter_context(nc.sbuf_tensor(name, shape, dt))

        W = {
            "cst": sbk("cst", [P, C_N]),
            "ident16": sbk("ident16", [P, P], f16),
            "br_all": sbk("br_all", [P, NF]),
            "wq_hi": sbk("wq_hi", [P, KC, D], f16), "wq_lo": sbk("wq_lo", [P, KC, D], f16),
            "wo_hi": sbk("wo_hi", [P, KC, D], f16), "wo_lo": sbk("wo_lo", [P, KC, D], f16),
            "wkv_hi": sbk("wkv_hi", [P, KC, 512], f16), "wkv_lo": sbk("wkv_lo", [P, KC, 512], f16),
            "aw_hi": sbk("aw_hi", [P, KC, AW], f16), "aw_lo": sbk("aw_lo", [P, KC, AW], f16),
            "bm_hi": sbk("bm_hi", [P, D], f16), "bm_lo": sbk("bm_lo", [P, D], f16),
        }
        s4_stage(nc, x, log_dt, lam, wq, wk, wv, wo, fa, fb, wr, br, consts, h0, W)
        layer_stage(nc, h0, out, W)


V_Z, V_X, V_F, N_PRE = 8, 14, 19, 54


def s4_stage(nc, x, log_dt, lam, wq, wk, wv, wo, fa, fb, wr, br, consts, h0, W):
    with ExitStack() as ctx:
        def sb(name, shape, dt=f32):
            return ctx.enter_context(nc.sbuf_tensor(name, shape, dt))

        def sem(name):
            return ctx.enter_context(nc.semaphore(name))

        cst = W["cst"]
        ident = cst[:, C_IDENT:C_IDENT + P]
        re_row, im_row, neg_re_row, row_sign = (cst[:, c:c + 1] for c in (C_RE, C_IM, C_NRE, C_SIGN))

        z = [[sb(f"z{i}{j}", [P, 2, HALF]) for j in range(2)] for i in range(ZR)]

        lam_p = sb("lam_p", [P, 2])
        gt0 = sb("gt0", [P, 1])
        le0 = sb("le0", [P, 1])
        sgn = sb("sgn", [P, 1])
        off = sb("off", [P, 2])
        pos = sb("pos", [P, NPOS])
        zr = sb("zr", [P, T])
        zi = sb("zi", [P, T])
        rr = sb("rr", [P, T])
        ss = sb("ss", [P, T])
        top_r = [sb(f"top_r{i}", [P, T]) for i in range(2)]
        top_i = [sb(f"top_i{i}", [P, T]) for i in range(2)]
        b0, b1, b2, b3, b4, b5 = (z[i][j][:, :, :].rearrange("p s l -> p (s l)") for i in range(3) for j in range(2))

        def part(buf, at, n):
            return buf[:, at:at + n]

        def rows(buf, at, n):
            return buf[:, at:at + n * T].rearrange("p (a t) -> p a t", a=n)

        ldt, dt, xr = part(b0, 0, 2 * T), part(b0, 2 * T, 2 * T), rows(b0, 4 * T, 3)
        yi, pk, tau = rows(b1, 0, 3), rows(b1, 3 * T, 3), rows(b1, 6 * T, 2)
        pf, sy, nd_r = rows(b2, 0, 3), rows(b2, 3 * T, 3), rows(b2, 6 * T, 2)
        hy, nd_i, em = rows(b3, 0, 3), rows(b3, 3 * T, 2), rows(b3, 5 * T, 2)
        t0, t1, dr, di, gr, gi, q0, q1 = (part(b4, T * i, T) for i in range(8))
        t2, dden, mag, w_r, w_i = rows(b5, 0, 2), rows(b5, 2 * T, 2), part(b5, 4 * T, T), part(b5, 5 * T, T), part(b5, 6 * T, T)

        theta = sb("theta", [P, TC, NPOS])
        expo = sb("expo", [P, TC, NPOS])
        turns = sb("turns", [P, TC, NPOS])
        half = sb("half", [P, TC, NPOS])
        m1, m2, m3, m4 = (sb(f"m{i}", [P, TC, DIG]) for i in range(4))
        tab = [sb(f"tab{i}", [P, 2, TC, NPOS]) for i in range(2)]
        u = [sb(f"u{i}", [P, 2, TC, DIG]) for i in range(2)]

        xq = sb("xq", [P, PAIRS, P])
        xd = [sb(f"xd{i}", [P, PAIRS, 3, NS]) for i in range(2)]
        prod_r = [sb(f"prod_r{i}", [P, QUAD * P]) for i in range(2)]
        prod_i = [sb(f"prod_i{i}", [P, QUAD * P]) for i in range(2)]
        xw = [[sb(f"xw{i}{j}", [P, QUAD * P]) for j in range(2)] for i in range(2)]
        hout = [sb(f"hout{i}", [P, D]) for i in range(2)]
        wst = [sb(f"wst{i}", [P, D]) for i in range(2)]
        fa_st, wr_st = hout[0], hout[1][0:NF, :]
        fb_st = wst[1][:, :].rearrange("p (k q) -> p k q", k=KC)

        hps = [[ctx.enter_context(nc.psum_tensor(f"hps{i}{j}", [P, 512], f32)) for j in range(2)] for i in range(2)]
        xps = [[ctx.enter_context(nc.psum_tensor(f"xps{i}{j}", [P, 512], f32)) for j in range(2)] for i in range(2)]
        fps = [hps[0][0], hps[0][1], hps[1][0], hps[1][1], xps[1][0]]

        small_in = sem("small_in")
        pre_v = sem("pre_v")
        pre_a = sem("pre_a")
        x_in = sem("x_in")
        xd_done = sem("xd_done")
        w_in = [sem(f"w_in{i}") for i in range(2)]
        w_hi = sem("w_hi")
        w_lo = sem("w_lo")
        ffn_in = sem("ffn_in")
        ffn_t = sem("ffn_t")
        ffn_hi = sem("ffn_hi")
        ffn_lo = sem("ffn_lo")
        tab_v = sem("tab_v")
        tab_a = sem("tab_a")
        tab_p = sem("tab_p")
        z_v = sem("z_v")
        z_p = sem("z_p")
        z_t = sem("z_t")
        z_used = sem("z_used")
        h_copied = sem("h_copied")
        xt_ps = sem("xt_ps")
        xw_v = sem("xw_v")
        h_sent = [sem(f"h_sent{i}") for i in range(2)]

        TV, TA, TP = 11, 4, 5
        x_v = x.rearrange("c (j s) n r -> s c j (n r)", s=2)
        h_v = h0.rearrange("c (j s) l -> s c j l", s=2)
        W_ITEMS = (("wq", D), ("wo", D), ("wkv", 512))
        W_COUNT = (16, 16, 48, 32, 64, 64)

        def ffn_parts(n, which):
            at, scaled = fps[n][:, :], (z[3][n // 2][:, n % 2, :] if n < 4 else xw[1][0][:, :])
            if n == 2:
                at, scaled = ((a[:, 0:KC * NF].rearrange("p (k h) -> p k h", k=KC)) for a in (at, scaled))
                return W["aw_" + which][:, :, P:AW], at, scaled
            if n < 2:
                at, scaled = ((a.rearrange("p (k h) -> p k h", k=4)) for a in (at, scaled))
                return W["aw_" + which][:, 4 * n:4 * n + 4, 0:P], at, scaled
            return W["bm_" + which][:, 512 * (n - 3):512 * (n - 2)], at, scaled

        def table(eng, k, j, s, ring):
            return eng.tensor_tensor(
                z[j % ZR][s][:, :, :].rearrange("p m (a b) -> p m a b", a=DIG),
                u[ring][:, :, 2 * j + s, :].unsqueeze(3).broadcast_to([P, 2, DIG, SEG]),
                tab[ring][:, :, 2 * j + s, DIG:].unsqueeze(2).broadcast_to([P, 2, DIG, SEG]), ALU.mult)

        with nc.Block() as block:
            @block.sync
            def _(sp):
                sp.dma_start(ldt, log_dt.rearrange("t r -> (t r)").partition_broadcast(P)).then_inc(small_in, 16)
                for r in range(2):
                    sp.dma_start(lam_p[r * NS:(r + 1) * NS, :], lam).then_inc(small_in, 16)
                sp.dma_start(cst[:, :], consts).then_inc(small_in, 16)
                sp.dma_start(W["br_all"][:, :], br.partition_broadcast(P)).then_inc(small_in, 16)
                for i in range(2):
                    sp.sem_inc(h_sent[i], 32)

                def load_x(k):
                    for s in range(2):
                        sp.dma_start(xq[64 * s:64 * s + 64, :, :],
                                     x_v[s, :, bass.ds(k * PAIRS, PAIRS), :]).then_inc(x_in, 16)

                def chunk(cc, h, last):
                    k = 2 * cc + h
                    if not last:
                        sp.wait_ge(xd_done, k + 1)
                        load_x(k + 1)
                    rows_ = bass.ds(k * P, P)
                    srcs = (((0, wq),), ((0, wo),), ((0, wk), (256, wv)))
                    for j in range(PAIRS):
                        if j in (0, 2, 4):
                            n = j // 2
                            sp.wait_ge(w_lo, 3 * k + n + 1)
                            ring = (3 * h + n) % 2
                            for at, src in srcs[n]:
                                sp.dma_start(wst[ring][:, at:at + src.shape[1]],
                                             src[rows_, :]).then_inc(w_in[ring], 16)
                        pair = k * PAIRS + j
                        sp.wait_ge(h_copied, 2 * pair + 6)
                        for s in range(2):
                            sp.dma_start(h_v[s, :, bass.ds(pair, 1), :].rearrange("c j l -> c (j l)"),
                                         hout[j % 2][64 * s:64 * s + 64, :]).then_inc(h_sent[j % 2], 16)

                load_x(0)
                sp.dma_start(fa_st[:, :], fa.rearrange("h r d -> (h r) d")).then_inc(ffn_in, 16)
                sp.dma_start(wr_st[:, :], wr).then_inc(ffn_in, 16)
                for h in range(NF):
                    sp.dma_start(fb_st[:, :, h * R:(h + 1) * R],
                                 fb[h].rearrange("(k p) r -> p k r", p=P)).then_inc(ffn_in, 16)
                with sp.Fori(0, CHUNKS // 2 - 1) as cc:
                    chunk(cc, 0, False)
                    chunk(cc, 1, False)
                chunk(CHUNKS // 2 - 1, 0, False)
                chunk(CHUNKS // 2 - 1, 1, True)
                for i in range(2):
                    sp.wait_ge(h_sent[i], 32 * (T // 4) + 32)

            @block.gpsimd
            def _(pool):
                pool.sem_inc(z_p, 1)

                def exponents(k):
                    nc.gpsimd.tensor_tensor(expo[:, :, :],
                                            zr[:, bass.ds(k * TC, TC)].unsqueeze(2).broadcast_to([P, TC, NPOS]),
                                            pos[:, :].unsqueeze(1).broadcast_to([P, TC, NPOS]),
                                            ALU.mult).then_inc(tab_p, 1)

                def table_i(k, ring, first):
                    pool.wait_ge(tab_a, TA * k + 3)
                    if not first:
                        pool.wait_ge(z_v, (k - 1) * PAIRS + 1)
                    nc.gpsimd.tensor_tensor(tab[ring][:, 1, :, :], expo[:, :, :], theta[:, :, :],
                                            ALU.mult).then_inc(tab_p, 1)

                def digits_i(k, ring):
                    rr_b, ss_b = (a[:, bass.ds(k * TC, TC)].unsqueeze(2).broadcast_to([P, TC, DIG]) for a in (rr, ss))
                    pool.wait_ge(tab_v, TV * k + 8)
                    nc.gpsimd.tensor_tensor(m3[:, :, :], ss_b, tab[ring][:, 0, :, 0:DIG], ALU.mult).then_inc(tab_p, 1)
                    pool.wait_ge(tab_p, TP * k + 2)
                    nc.gpsimd.tensor_tensor(m4[:, :, :], rr_b, tab[ring][:, 1, :, 0:DIG], ALU.mult).then_inc(tab_p, 1)
                    pool.wait_ge(tab_p, TP * k + 4)
                    nc.gpsimd.tensor_tensor(u[ring][:, 1, :, :], m3[:, :, :], m4[:, :, :],
                                            ALU.subtract).then_inc(tab_p, 1)

                def chunk(cc, h, last):
                    k = 2 * cc + h
                    for j in range(PAIRS):
                        if j == 0:
                            pool.wait_ge(tab_p, TP * k + 5)
                            pool.wait_ge(tab_v, TV * k + 11)
                        pool.wait_ge(z_used, k * PAIRS + j + 1)
                        made = table(nc.gpsimd, k, j, 1, h)
                        if j not in SUMMED:
                            made.then_inc(z_p, 1)
                        else:
                            made.then_inc(z_t, 1)
                            pool.wait_ge(z_t, len(SUMMED) * k + SUMMED.index(j) + 1)
                            pool.wait_ge(z_v, k * PAIRS + j + 2)
                            for s in range(2):
                                zs = z[j % ZR][s]
                                made = nc.gpsimd.tensor_tensor(zs[:, 0, :], zs[:, 0, :], zs[:, 1, :], ALU.add)
                            made.then_inc(z_p, 1)
                        if j == 0 and not last:
                            exponents(k + 1)
                        if j == 5 and not last:
                            table_i(k + 1, (h + 1) % 2, False)
                            digits_i(k + 1, (h + 1) % 2)

                pool.wait_ge(pre_v, V_Z)
                exponents(0)
                table_i(0, 0, True)
                for n in range(5):
                    pool.wait_ge(ffn_hi, n + 1)
                    hi, _, scaled = ffn_parts(n, "hi")
                    lo = ffn_parts(n, "lo")[0]
                    nc.gpsimd.tensor_tensor(lo, scaled, hi, ALU.subtract).then_inc(ffn_lo, 1)
                pool.wait_ge(pre_v, N_PRE)
                digits_i(0, 0)
                with pool.Fori(0, CHUNKS // 2 - 1) as cc:
                    chunk(cc, 0, False)
                    chunk(cc, 1, False)
                chunk(CHUNKS // 2 - 1, 0, False)
                chunk(CHUNKS // 2 - 1, 1, True)

            @block.scalar
            def _(act):
                act.sem_inc(h_copied, 4)

                def exps(k):
                    act.wait_ge(tab_p, TP * k + 1)
                    nc.scalar.activation(expo[:, :, :], expo[:, :, :], ACT.Exp).then_inc(tab_a, 1)

                def sines(k):
                    act.wait_ge(tab_v, TV * k + 6)
                    nc.scalar.activation(half[:, :, :], theta[:, :, :], ACT.Sin, scale=0.5).then_inc(tab_a, 1)
                    act.wait_ge(tab_a, TA * k + 2)
                    nc.scalar.activation(theta[:, :, :], theta[:, :, :], ACT.Sin).then_inc(tab_a, 1)
                    nc.scalar.activation(half[:, :, :], half[:, :, :], ACT.Square).then_inc(tab_a, 1)

                def split_x(k, ring, first):
                    act.wait_ge(x_in, 32 * k + 32)
                    if not first:
                        act.wait_ge(xt_ps, 2 * k - 1)
                    parts = xq[:, :, :].rearrange("p j (n r) -> p j n r", r=2)
                    for n in range(3):
                        last = nc.scalar.activation(xd[ring][:, :, n, :], parts[:, :, :, n % 2], ACT.Copy)
                    last.then_inc(xd_done, 1)

                def weight_hi(cc, h, n):
                    k, ring = 2 * cc + h, (3 * h + n) % 2
                    name, width = W_ITEMS[n]
                    act.wait_ge(w_in[ring], 64 * cc + W_COUNT[3 * h + n])
                    nc.scalar.activation(W[name + "_hi"][:, bass.ds(k, 1), :].rearrange("p k n -> p (k n)"),
                                         wst[ring][:, 0:width], ACT.Copy, scale=WS).then_inc(w_hi, 1)

                def chunk(cc, h, last):
                    k = 2 * cc + h
                    for j in range(PAIRS):
                        if j == 0 and not last:
                            exps(k + 1)
                            sines(k + 1)
                        if j == 1 and not last:
                            split_x(k + 1, (h + 1) % 2, False)
                        if j in (2, 4, 5):
                            weight_hi(cc, h, (2, 4, 5).index(j))
                        pair = k * PAIRS + j
                        act.wait_ge(z_used, pair + ZR + 1)
                        act.wait_ge(h_sent[j % 2], 32 * (k * PAIRS // 2 + j // 2) + 32)
                        for n in range(2):
                            nc.scalar.activation(hout[j % 2][:, n * HALF:(n + 1) * HALF], hps[j % 2][n][:, :],
                                                 ACT.Copy).then_inc(h_copied, 1)

                act.wait_ge(small_in, 80)
                nc.scalar.activation(dt, ldt, ACT.Exp).then_inc(pre_a, 1)
                act.wait_ge(pre_v, V_X)
                nc.scalar.activation(mag, xr[:, 2, :], ACT.Exp).then_inc(pre_a, 1)
                exps(0)
                nc.scalar.activation(tau, xr[:, 0:2, :], ACT.Tanh, scale=0.5).then_inc(pre_a, 1)
                act.wait_ge(pre_v, V_F)
                nc.scalar.activation(sy, pf, ACT.Sin).then_inc(pre_a, 1)
                nc.scalar.activation(hy, pf, ACT.Sin, scale=0.5).then_inc(pre_a, 1)
                sines(0)
                split_x(0, 0, True)
                for n in range(5):
                    act.wait_ge(ffn_t, n + 1)
                    dst, src, scaled = ffn_parts(n, "hi")
                    nc.scalar.activation(dst, src, ACT.Copy, scale=WS)
                    nc.scalar.activation(scaled, src, ACT.Copy, scale=WS).then_inc(ffn_hi, 1)
                with act.Fori(0, CHUNKS // 2 - 1) as cc:
                    chunk(cc, 0, False)
                    chunk(cc, 1, False)
                chunk(CHUNKS // 2 - 1, 0, False)
                chunk(CHUNKS // 2 - 1, 1, True)

            @block.vector
            def _(dve):
                V = nc.vector
                steps = [0]

                def step(*instructions):
                    for ins in instructions:
                        ins.then_inc(pre_v, 1)
                    steps[0] += len(instructions)
                    dve.wait_ge(pre_v, steps[0])

                def angles_a(k):
                    V.tensor_tensor(theta[:, :, :],
                                    zi[:, bass.ds(k * TC, TC)].unsqueeze(2).broadcast_to([P, TC, NPOS]),
                                    pos[:, :].unsqueeze(1).broadcast_to([P, TC, NPOS]),
                                    ALU.mult).then_inc(tab_v, 1)
                    dve.wait_ge(tab_v, TV * k + 1)
                    V.tensor_scalar(turns[:, :, :], theta[:, :, :], INV_2PI, MAGIC, ALU.mult, ALU.add).then_inc(tab_v, 1)
                    dve.wait_ge(tab_v, TV * k + 2)
                    V.tensor_scalar(turns[:, :, :], turns[:, :, :], MAGIC, None, ALU.subtract).then_inc(tab_v, 1)

                def angles_b(k):
                    dve.wait_ge(tab_v, TV * k + 3)
                    V.scalar_tensor_tensor(theta[:, :, :], turns[:, :, :], -TWO_PI_HI, theta[:, :, :],
                                           ALU.mult, ALU.add).then_inc(tab_v, 1)
                    dve.wait_ge(tab_v, TV * k + 4)
                    V.scalar_tensor_tensor(theta[:, :, :], turns[:, :, :], -TWO_PI_LO, theta[:, :, :],
                                           ALU.mult, ALU.add).then_inc(tab_v, 1)
                    dve.wait_ge(tab_v, TV * k + 5)
                    V.tensor_scalar(theta[:, :, :], theta[:, :, :], PI_SAFE, -PI_SAFE,
                                    ALU.min, ALU.max).then_inc(tab_v, 1)

                def table_r(k, ring, first):
                    dve.wait_ge(tab_a, TA * k + 4)
                    V.tensor_scalar(half[:, :, :], half[:, :, :], -2.0, 1.0, ALU.mult, ALU.add).then_inc(tab_v, 1)
                    dve.wait_ge(tab_v, TV * k + 7)
                    if not first:
                        dve.wait_ge(z_p, (k - 1) * PAIRS + 1)
                    V.tensor_tensor(tab[ring][:, 0, :, :], expo[:, :, :], half[:, :, :], ALU.mult).then_inc(tab_v, 1)

                def digits_r(k, ring):
                    rr_b, ss_b = (a[:, bass.ds(k * TC, TC)].unsqueeze(2).broadcast_to([P, TC, DIG]) for a in (rr, ss))
                    dve.wait_ge(tab_v, TV * k + 8)
                    V.tensor_tensor(m1[:, :, :], rr_b, tab[ring][:, 0, :, 0:DIG], ALU.mult).then_inc(tab_v, 1)
                    dve.wait_ge(tab_p, TP * k + 2)
                    V.tensor_tensor(m2[:, :, :], ss_b, tab[ring][:, 1, :, 0:DIG], ALU.mult).then_inc(tab_v, 1)
                    dve.wait_ge(tab_v, TV * k + 10)
                    V.tensor_tensor(u[ring][:, 0, :, :], m1[:, :, :], m2[:, :, :], ALU.add).then_inc(tab_v, 1)

                def top_factors(q, ring, first):
                    at = bass.ds(q * 2 * QUAD, 2 * QUAD)
                    dve.wait_ge(xt_ps, q + 1)
                    dve.wait_ge(xw_v, 2 * q + 4)
                    for top in range(2):
                        for prod, coef, src in ((prod_r, top_r, xps[ring][0]), (prod_i, top_i, xps[ring][1])):
                            last = V.tensor_tensor(prod[top][:, :].rearrange("p (t c) -> p t c", c=NB),
                                                   src[:, :].rearrange("p (t c) -> p t c", c=NB),
                                                   coef[top][:, at].unsqueeze(2).broadcast_to([P, 2 * QUAD, NB]),
                                                   ALU.mult)
                    last.then_inc(xw_v, 1)
                    dve.wait_ge(xw_v, 2 * q + 5)
                    if not first:
                        dve.wait_ge(z_used, q * QUAD)
                    for top in range(2):
                        last = V.tensor_tensor(xw[ring][top][:, :], prod_r[top][:, :], prod_i[top][:, :], ALU.add)
                    last.then_inc(xw_v, 1)

                def weight_lo(k, h, n):
                    ring = (3 * h + n) % 2
                    name, width = W_ITEMS[n]
                    dve.wait_ge(w_hi, 3 * k + n + 1)
                    hi, lo = (W[name + s][:, bass.ds(k, 1), :].rearrange("p k n -> p (k n)") for s in ("_hi", "_lo"))
                    V.scalar_tensor_tensor(lo, wst[ring][:, 0:width], WS, hi, ALU.mult, ALU.subtract).then_inc(w_lo, 1)

                def chunk(cc, h, last):
                    k = 2 * cc + h
                    for j in range(PAIRS):
                        if j == 0:
                            dve.wait_ge(tab_v, TV * k + 11)
                            dve.wait_ge(tab_p, TP * k + 5)
                        dve.wait_ge(z_used, k * PAIRS + j + 1)
                        table(V, k, j, 0, h).then_inc(z_v, 1)
                        if j == 2 and not last:
                            angles_a(k + 1)
                        if j == 3:
                            if not last:
                                angles_b(k + 1)
                            top_factors(2 * k + 1, 1, False)
                            if not last:
                                table_r(k + 1, (h + 1) % 2, False)
                        if j == 5:
                            weight_lo(k, h, 0)
                        if j == 6 and not last:
                            digits_r(k + 1, (h + 1) % 2)
                        if j == 7:
                            weight_lo(k, h, 1)
                            if not last:
                                top_factors(2 * k + 2, 0, False)
                            weight_lo(k, h, 2)

                dve.sem_inc(z_v, 1)
                dve.sem_inc(w_lo, 2)
                dve.sem_inc(xw_v, 4)
                dve.wait_ge(small_in, 80)
                step(V.tensor_scalar(gt0[:, :], lam_p[:, 0:1], 0.0, None, ALU.is_gt))
                step(V.tensor_scalar(off[:, :], cst[:, C_END:C_END + 2], gt0[:, :], None, ALU.mult),
                     V.tensor_scalar(sgn[:, :], gt0[:, :], -2.0, 1.0, ALU.mult, ALU.add),
                     V.tensor_scalar(le0[:, :], gt0[:, :], -1.0, 1.0, ALU.mult, ALU.add))
                dve.wait_ge(pre_a, 1)
                dt_v = dt.rearrange("p (t r) -> p t r", r=2)
                step(V.tensor_scalar(zr[:, :], dt_v[:, :, 0], lam_p[:, 0:1], None, ALU.mult),
                     V.tensor_scalar(zi[:, :], dt_v[:, :, 1], lam_p[:, 1:2], None, ALU.mult),
                     *[V.tensor_scalar(pos[:, at:at + n], cst[:, C_POS + at:C_POS + at + n],
                                       off[:, d:d + 1], None, ALU.add) for d, n, at in ((0, DIG, 0), (1, SEG, DIG))])
                assert steps[0] == V_Z
                lengths = (1.0, float(D), float(HALF))
                step(*[V.tensor_scalar(xr[:, n, :], zr[:, :], sgn[:, :], lengths[n], ALU.mult, ALU.mult)
                       for n in range(3)],
                     *[V.tensor_scalar(yi[:, n, :], zi[:, :], sgn[:, :], lengths[n], ALU.mult, ALU.mult)
                       for n in range(3)])
                assert steps[0] == V_X
                step(V.tensor_scalar(pk, yi, INV_2PI, MAGIC, ALU.mult, ALU.add))
                step(V.tensor_scalar(pk, pk, MAGIC, None, ALU.subtract))
                step(V.scalar_tensor_tensor(pf, pk, -TWO_PI_HI, yi, ALU.mult, ALU.add))
                step(V.scalar_tensor_tensor(pf, pk, -TWO_PI_LO, pf, ALU.mult, ALU.add))
                step(V.tensor_scalar(pf, pf, PI_SAFE, -PI_SAFE, ALU.min, ALU.max))
                assert steps[0] == V_F
                angles_a(0)
                angles_b(0)
                dve.wait_ge(pre_a, 5)
                step(V.tensor_scalar(dden, tau, -1.0, 1.0, ALU.mult, ALU.add),
                     V.tensor_tensor(hy, hy, hy, ALU.mult))
                step(V.reciprocal(dden, dden),
                     V.tensor_scalar(t2, hy[:, 0:2, :], -2.0, 1.0, ALU.mult, ALU.add),
                     V.tensor_scalar(w_r, hy[:, 2, :], -2.0, 1.0, ALU.mult, ALU.add),
                     V.tensor_tensor(w_i, sy[:, 2, :], mag, ALU.mult))
                step(V.scalar_tensor_tensor(em, tau, 2.0, dden, ALU.mult, ALU.mult),
                     V.tensor_tensor(w_r, w_r, mag, ALU.mult))
                step(V.tensor_tensor(t2, em, t2, ALU.mult),
                     V.scalar_tensor_tensor(nd_i, em, 1.0, sy[:, 0:2, :], ALU.add, ALU.mult),
                     V.tensor_scalar(top_r[0][:, :], w_r, gt0[:, :], le0[:, :], ALU.mult, ALU.add),
                     V.tensor_scalar(top_i[0][:, :], w_i, gt0[:, :], row_sign, ALU.mult, ALU.mult))
                step(V.scalar_tensor_tensor(nd_r, hy[:, 0:2, :], -2.0, t2, ALU.mult, ALU.add),
                     V.tensor_scalar(top_r[1][:, :], w_r, le0[:, :], gt0[:, :], ALU.mult, ALU.add),
                     V.tensor_scalar(top_i[1][:, :], w_i, le0[:, :], row_sign, ALU.mult, ALU.mult),
                     V.tensor_scalar(t0, nd_i[:, 1, :], lam_p[:, 1:2], None, ALU.mult),
                     V.tensor_scalar(t1, nd_i[:, 1, :], lam_p[:, 0:1], None, ALU.mult))
                step(V.scalar_tensor_tensor(dr, nd_r[:, 1, :], lam_p[:, 0:1], t0, ALU.mult, ALU.subtract),
                     V.scalar_tensor_tensor(di, nd_r[:, 1, :], lam_p[:, 1:2], t1, ALU.mult, ALU.add))
                step(V.tensor_tensor(q0, dr, dr, ALU.mult),
                     V.tensor_tensor(q1, di, di, ALU.mult),
                     V.tensor_tensor(t0, nd_r[:, 0, :], dr, ALU.mult),
                     V.tensor_tensor(t1, nd_i[:, 0, :], di, ALU.mult))
                step(V.scalar_tensor_tensor(q0, q0, RECIP_EPS, q1, ALU.add, ALU.add),
                     V.tensor_tensor(gr, t0, t1, ALU.add))
                step(V.reciprocal(q0, q0),
                     V.tensor_tensor(t0, nd_i[:, 0, :], dr, ALU.mult),
                     V.tensor_tensor(t1, nd_r[:, 0, :], di, ALU.mult))
                step(V.tensor_tensor(gr, gr, q0, ALU.mult),
                     V.tensor_tensor(gi, t0, t1, ALU.subtract))
                step(V.tensor_tensor(gi, gi, q0, ALU.mult),
                     V.tensor_scalar(t1, gr, im_row, None, ALU.mult))
                step(V.tensor_scalar(t0, gi, im_row, None, ALU.mult),
                     V.scalar_tensor_tensor(ss[:, :], gi, neg_re_row, t1, ALU.mult, ALU.subtract))
                step(V.scalar_tensor_tensor(rr[:, :], gr, re_row, t0, ALU.mult, ALU.subtract))
                assert steps[0] == N_PRE
                table_r(0, 0, True)
                digits_r(0, 0)
                top_factors(0, 0, True)
                V.tensor_copy(W["ident16"][:, :], ident)
                dve.wait_ge(ffn_lo, 5)
                with dve.Fori(0, CHUNKS // 2 - 1) as cc:
                    chunk(cc, 0, False)
                    chunk(cc, 1, False)
                chunk(CHUNKS // 2 - 1, 0, False)
                chunk(CHUNKS // 2 - 1, 1, True)

            @block.tensor
            def _(pe):
                def transposes(k, h, q, ring):
                    pe.wait_ge(xd_done, k + 1)
                    pe.wait_ge(xw_v, 2 * q + 1)
                    for swap in range(2):
                        for j in range(QUAD):
                            parts = xd[h][:, QUAD * ring + j, swap:swap + 2, :].rearrange("p r n -> p (r n)")
                            last = pe.transpose(xps[ring][swap][:, j * P:(j + 1) * P], parts, ident)
                    last.then_inc(xt_ps, 1)

                def pairs(k, q, ring):
                    pe.wait_ge(xw_v, 2 * q + 6)
                    for j in range(QUAD * ring, QUAD * ring + QUAD):
                        pair = k * PAIRS + j
                        pe.wait_ge(z_v, pair + 2)
                        pe.wait_ge(z_p, pair + 2)
                        pe.wait_ge(h_copied, 2 * pair + 2)
                        parts = 1 if j in SUMMED else 2
                        for top in range(2):
                            for m in range(parts):
                                for s in range(2):
                                    at = (j % QUAD) * P + NB * s
                                    last = pe.matmul(hps[j % 2][top][NB * s:NB * s + NB, :],
                                                     xw[ring][top][:, at:at + NB],
                                                     z[j % ZR][s][:, m, :], start=(m == 0), stop=(m == parts - 1))
                        last.then_inc(z_used, 1)

                def chunk(cc, h, last):
                    k = 2 * cc + h
                    transposes(k, h, 2 * k + 1, 1)
                    pairs(k, 2 * k, 0)
                    if not last:
                        transposes(k + 1, (h + 1) % 2, 2 * k + 2, 0)
                    pairs(k, 2 * k + 1, 1)

                pe.sem_inc(z_used, ZR)
                pe.wait_ge(small_in, 80)
                pe.wait_ge(ffn_in, 16 * (2 + NF))
                for n in range(5):
                    for k in range(KC if n == 2 else 4):
                        if n == 2:
                            last = pe.transpose(fps[n][:, k * NF:(k + 1) * NF], wr_st[:, k * P:(k + 1) * P],
                                                ident[0:NF, 0:NF])
                        elif n < 2:
                            at = (4 * n + k) * P
                            last = pe.transpose(fps[n][:, k * P:(k + 1) * P], fa_st[:, at:at + P], ident)
                        else:
                            last = pe.transpose(fps[n][:, k * P:(k + 1) * P], fb_st[:, 4 * (n - 3) + k, :], ident)
                    last.then_inc(ffn_t, 1)
                transposes(0, 0, 0, 0)
                pe.wait_ge(ffn_hi, 5)
                with pe.Fori(0, CHUNKS // 2 - 1) as cc:
                    chunk(cc, 0, False)
                    chunk(cc, 1, False)
                chunk(CHUNKS // 2 - 1, 0, False)
                chunk(CHUNKS // 2 - 1, 1, True)


def layer_stage(nc, h0, out, W):
    with ExitStack() as ctx:
        def sb(name, shape, dt=f32):
            return ctx.enter_context(nc.sbuf_tensor(name, shape, dt))

        def sem(name):
            return ctx.enter_context(nc.semaphore(name))

        cst, ident16 = W["cst"], W["ident16"]
        ident = cst[:, C_IDENT:C_IDENT + P]
        mask = cst[:, C_MASK:C_MASK + P]

        h_ln = sb("h_ln", [P, D])
        h_res = sb("h_res", [P, D])
        xn = [sb(f"xn{i}", [P, D]) for i in range(2)]
        xt_hi = [sb(f"xt_hi{i}", [P, KC, P], f16) for i in range(2)]
        xt_lo = [sb(f"xt_lo{i}", [P, KC, P], f16) for i in range(2)]
        bn = [sb(f"bn{i}", [P, 12]) for i in range(2)]
        mv = [sb(f"mv{i}", [P, 2]) for i in range(2)]
        nrm = [sb(f"nrm{i}", [P, 8]) for i in range(2)]
        rt_c = sb("rt_c", [P, 512])
        rt_s = sb("rt_s", [P, 512])
        qr = sb("qr", [P, 512])
        qs = sb("qs", [P, H, 2, 2, HD], f16)
        kt_c = sb("kt_c", [P, G * HD])
        kt_s = sb("kt_s", [P, G * HD])
        kr = sb("kr", [P, G * HD])
        ks = sb("ks", [P, G, 2, 2, HD], f16)
        vf = sb("vf", [P, G * HD])
        v_hi = sb("v_hi", [P, G * HD], f16)
        v_lo = sb("v_lo", [P, G * HD], f16)
        qt = [sb(f"qt{i}", [P, HG * P], f16) for i in range(2)]
        kt = sb("kt", [P, G, P], f16)
        sm = [sb(f"sm{i}", [P, HG * P]) for i in range(2)]
        smin = [sb(f"smin{i}", [P, HG]) for i in range(2)]
        pr = [sb(f"pr{i}", [P, HG * P]) for i in range(2)]
        rsum = [sb(f"rsum{i}", [P, HG]) for i in range(2)]
        rinv = [sb(f"rinv{i}", [P, HG]) for i in range(2)]
        pt_hi = sb("pt_hi", [P, HG * P], f16)
        pt_lo = sb("pt_lo", [P, HG * P], f16)
        ctx_hi = sb("ctx_hi", [P, G, P], f16)
        ctx_lo = sb("ctx_lo", [P, G, P], f16)
        h1 = sb("h1", [P, D])
        z8 = sb("z8", [P, NF])
        e8 = sb("e8", [P, NF])
        w8 = sb("w8", [P, NF])
        s8 = sb("s8", [P, 4])
        ls = sb("ls", [P, P])
        ls_hi = sb("ls_hi", [P, P], f16)
        ls_lo = sb("ls_lo", [P, P], f16)
        h2 = sb("h2", [P, D])

        s_ps = ctx.enter_context(nc.psum_tensor("s_ps", [P, 512], f32))
        pt_ps = ctx.enter_context(nc.psum_tensor("pt_ps", [P, 512], f32))
        pv_ps = ctx.enter_context(nc.psum_tensor("pv_ps", [P, 512], f32))
        pa = ctx.enter_context(nc.psum_tensor("pa", [P, 512], f32))
        pb = ctx.enter_context(nc.psum_tensor("pb", [P, 512], f32))
        pc = ctx.enter_context(nc.psum_tensor("pc", [P, 512], f32))
        tq = ctx.enter_context(nc.psum_tensor("tq", [P, 1024], f16))
        tx = ctx.enter_context(nc.psum_tensor("tx", [P, 512], f32))
        tx16 = tx[:, :].bitcast(f16)

        ln_in = sem("ln_in")
        res_in = sem("res_in")
        out_sent = sem("out_sent")
        s_done = sem("s_done")
        qt_done = sem("qt_done")
        pt_done = sem("pt_done")
        pv_done = sem("pv_done")
        kv_done = sem("kv_done")
        q_done = sem("q_done")
        wo_done = sem("wo_done")
        ctx_used = sem("ctx_used")
        low_done = sem("low_done")
        out_done = sem("out_done")
        xt_done = [sem(f"xt_done{i}") for i in range(2)]
        kt_done = sem("kt_done")
        lst_done = sem("lst_done")
        qt_copied = sem("qt_copied")
        kt_copied = sem("kt_copied")
        exp_done = sem("exp_done")
        pth_done = sem("pth_done")
        ctxh_done = sem("ctxh_done")
        ln_y = [sem(f"ln_y{i}") for i in range(2)]
        ln_x = [sem(f"ln_x{i}") for i in range(2)]
        xth_done = [sem(f"xth_done{i}") for i in range(2)]
        low_e = sem("low_e")
        lsh_done = sem("lsh_done")
        qh_done = sem("qh_done")
        kh_done = sem("kh_done")
        vh_done = sem("vh_done")
        waits_held = sem("waits_held")
        masked = sem("masked")
        rinv_done = sem("rinv_done")
        ptl_done = sem("ptl_done")
        ctxl_done = sem("ctxl_done")
        ln_v = [sem(f"ln_v{i}") for i in range(2)]
        xtl_done = [sem(f"xtl_done{i}") for i in range(2)]
        kv_used = sem("kv_used")
        q_used = sem("q_used")
        h1_done = sem("h1_done")
        h2_done = sem("h2_done")
        low_v = sem("low_v")
        lsl_done = sem("lsl_done")
        qd_done = sem("qd_done")
        kd_done = sem("kd_done")
        q_sum = sem("q_sum")
        ql_done = sem("ql_done")
        k_sum = sem("k_sum")
        kl_done = sem("kl_done")
        vl_done = sem("vl_done")
        p_norm = sem("p_norm")

        FIRST, LAST = 3, NB - 3

        def has(b):
            return not isinstance(b, int) or 0 <= b < NB

        def reached(eng, s, per, b, k=0):
            if isinstance(b, int):
                if b < 0 or per * b + k == 0:
                    return
                if b >= NB:
                    b, k = NB, 0
            eng.wait_ge(s, per * b + k)

        def hold_waits(dve):
            dve.sem_inc(waits_held, 1)

        def group(i, s):
            return (i - 1, s + G) if s < 0 else (i + 1, s - G) if s >= G else (i, s)

        def bank_free(pe, i, tiles, n):
            for m, (s, per, ahead, k) in enumerate(tiles):
                if isinstance(i, int) or m == (n - 1) % len(tiles):
                    reached(pe, s, per, i + ahead - (m >= n), k)

        def wo_free(eng, b, g):
            if g < KC - 1:
                reached(eng, ctx_used, KC - 1, b - 1, g + 1)
            else:
                reached(eng, wo_done, 2, b)

        PA = ((kv_used, 1, 1, 1), (h1_done, 2, -1, 1), (q_used, 2, 1, 2))
        PB = ((h2_done, 2, -2, 1), (h1_done, 2, -1, 2), (low_v, 5, -1, 5))
        PC = ((h2_done, 2, -2, 2), (q_used, 2, 1, 1))
        TX = ((xtl_done[0], 2, 1, 2), (lsl_done, 1, -2, 1), (kt_copied, 2, 1, 1), (xtl_done[1], 2, -1, 1),
              (xtl_done[1], 2, -1, 2), (kt_copied, 2, 1, 2), (xtl_done[0], 2, 2, 1))

        def bodies(eng, body):
            for i in range(-2, FIRST):
                body(i)
            with eng.Fori(FIRST, LAST) as i:
                body(i)
            for i in range(LAST, NB + 2):
                body(i)

        with nc.Block() as block:
            @block.sync
            def _(sp):
                def row(ap, b):
                    return ap[bass.ds(b, 1), :, :].rearrange("b t d -> (b t) d")

                def body(i):
                    if has(i - 1):
                        reached(sp, h1_done, 2, i - 1)
                        sp.dma_start(h_res[:, :], row(h0, i - 1)).then_inc(res_in, 16)
                    if has(i - 2):
                        reached(sp, h2_done, 2, i - 2, 2)
                        sp.dma_start(row(out, i - 2), h2[:, :]).then_inc(out_sent, 16)
                    if has(i + 3):
                        reached(sp, ln_x[0], 1, i + 2, 1)
                        sp.dma_start(h_ln[:, :], row(h0, i + 3)).then_inc(ln_in, 16)

                sp.dma_start(h_ln[:, :], row(h0, 0)).then_inc(ln_in, 16)
                bodies(sp, body)
                sp.wait_ge(out_sent, 16 * NB)

            @block.tensor
            def _(pe):
                def products(ps, x_hi, x_lo, name, cols, k0, k1):
                    w_hi, w_lo = W[name + "_hi"], W[name + "_lo"]
                    for k in range(k0, k1):
                        pe.matmul(ps, x_hi[:, k, :], w_hi[:, k, cols], start=(k == 0), stop=False)
                        pe.matmul(ps, x_hi[:, k, :], w_lo[:, k, cols], start=False, stop=False)
                        last = pe.matmul(ps, x_lo[:, k, :], w_hi[:, k, cols], start=False, stop=(k == KC - 1))
                    return last

                def scores(i, s):
                    if not has(i):
                        return
                    reached(pe, qt_copied, G, i, s + 1)
                    if s == 0 or s == G // 2:
                        reached(pe, kt_copied, 2, i, 1 + s // (G // 2))
                    reached(pe, masked, 4 * G, i, 4 * s)
                    for j in range(HG):
                        last = pe.matmul(s_ps[:, j * P:(j + 1) * P], qt[s % 2][:, j * P:(j + 1) * P],
                                         kt[:, s, :], start=True, stop=True)
                    last.then_inc(s_done, 1)

                def q_transpose(b, g):
                    if not has(b):
                        return
                    reached(pe, qd_done, 2, b, 1 + g // (G // 2))
                    reached(pe, qt_copied, G, b, g)
                    for j in range(HG):
                        last = pe.transpose(tq[:, j * P:(j + 1) * P],
                                            qs[:, HG * g + j, :, :, :].rearrange("p a b d -> p (a b d)"),
                                            ident16[:, :])
                    last.then_inc(qt_done, 1)

                def p_transpose(b, g):
                    if not has(b):
                        return
                    reached(pe, p_norm, G, b, g + 1)
                    reached(pe, ptl_done, G, b, g)
                    for j in range(HG):
                        last = pe.transpose(pt_ps[:, j * P:(j + 1) * P], pr[g % 2][:, j * P:(j + 1) * P], ident)
                    last.then_inc(pt_done, 1)

                def values(b, g):
                    if not has(b):
                        return
                    reached(pe, ptl_done, G, b, g + 1)
                    reached(pe, vl_done, 1, b, 1)
                    reached(pe, ctxl_done, G, b, g)
                    for n, (v, pt) in enumerate(((v_hi, pt_hi), (v_lo, pt_hi), (v_hi, pt_lo))):
                        for j in range(HG):
                            last = pe.matmul(pv_ps[j * HD:(j + 1) * HD, 0:P], v[:, g * HD:(g + 1) * HD],
                                             pt[:, j * P:(j + 1) * P], start=(n == 0), stop=(n == 2))
                    last.then_inc(pv_done, 1)

                def x_transpose(w, b, tile, i, n):
                    if not has(b):
                        return
                    reached(pe, ln_x[w], 1, b, 1)
                    bank_free(pe, i, TX, n)
                    for j in range(4):
                        at = (4 * tile + j) * P
                        last = pe.transpose(tx[:, j * P:(j + 1) * P], xn[w][:, at:at + P], ident)
                    last.then_inc(xt_done[w], 1)

                def k_transpose(b, tile, i, n):
                    if not has(b):
                        return
                    reached(pe, kd_done, 1, b, 1)
                    bank_free(pe, i, TX, n)
                    for j in range(4):
                        last = pe.transpose(tx16[:, j * P:(j + 1) * P],
                                            ks[:, 4 * tile + j, :, :, :].rearrange("p a b d -> p (a b d)"),
                                            ident16[:, :])
                    last.then_inc(kt_done, 1)

                def kv(i, k0, k1):
                    if not has(i + 1):
                        return
                    if k0 == 0:
                        bank_free(pe, i, PA, 0)
                    reached(pe, xtl_done[0], 2, i + 1, 1 + (k1 > 4))
                    last = products(pa[:, :], xt_hi[0], xt_lo[0], "wkv", slice(0, 512), k0, k1)
                    if k1 == KC:
                        last.then_inc(kv_done, 1)

                def q_half(i, half, k0, k1):
                    if not has(i + 1):
                        return
                    if k0 == 0:
                        bank_free(pe, i, (PC, PA)[half], (1, 2)[half])
                    last = products((pc, pa)[half][:, :], xt_hi[0], xt_lo[0], "wq",
                                    slice(512 * half, 512 * half + 512), k0, k1)
                    if k1 == KC:
                        last.then_inc(q_done, 1)

                def out_half(i, half):
                    if not has(i - 2):
                        return
                    reached(pe, lsl_done, 1, i - 2, 1)
                    bank_free(pe, i, (PB, PC)[half], 0)
                    ps, cols = (pb, pc)[half], slice(512 * half, 512 * half + 512)
                    pe.matmul(ps[:, :], ls_hi[:, :], W["bm_hi"][:, cols], start=True, stop=False)
                    pe.matmul(ps[:, :], ls_hi[:, :], W["bm_lo"][:, cols], start=False, stop=False)
                    pe.matmul(ps[:, :], ls_lo[:, :], W["bm_hi"][:, cols], start=False, stop=True).then_inc(out_done, 1)

                def wo_half(i, half, k0, k1):
                    if not has(i - 1):
                        return
                    if k0 == 0:
                        bank_free(pe, i, (PA, PB)[half], 1)
                    for k in range(k0, k1):
                        if half == 0:
                            reached(pe, ctxl_done, G, i - 1, k + 1)
                        last = products((pa, pb)[half][:, :], ctx_hi, ctx_lo, "wo",
                                        slice(512 * half, 512 * half + 512), k, k + 1)
                        if half == 1 and k < KC - 1:
                            last.then_inc(ctx_used, 1)
                    if k1 == KC:
                        last.then_inc(wo_done, 1)

                def low(i, k0, k1):
                    if not has(i - 1):
                        return
                    if k0 == 0:
                        bank_free(pe, i, PB, 2)
                        reached(pe, xtl_done[1], 2, i - 1, 2)
                    last = products(pb[:, 0:AW], xt_hi[1], xt_lo[1], "aw", slice(0, AW), k0, k1)
                    if k1 == KC:
                        last.then_inc(low_done, 1)

                def ls_transpose(i):
                    if not has(i - 2):
                        return
                    reached(pe, low_v, 5, i - 2, 5)
                    bank_free(pe, i, TX, 1)
                    pe.transpose(tx[:, 0:P], ls[:, :], ident).then_inc(lst_done, 1)

                def body(i):
                    for s in range(G):
                        scores(i, s)
                        if s == 2:
                            wo_half(i, 0, 0, 2)
                        if s == 3:
                            wo_half(i, 1, 2, 3)
                        if s == 6:
                            q_half(i, 0, 6, 8)
                        if s == 7:
                            x_transpose(1, i - 1, 1, i, 4)
                        q_transpose(*group(i, s + 1))
                        if s == 2:
                            wo_half(i, 0, 2, 3)
                        if s == 4:
                            wo_half(i, 1, 4, 6)
                        if s == 5:
                            q_half(i, 0, 1, 3)
                        if s == 6:
                            q_half(i, 1, 0, 2)
                        values(*group(i, s - 2))
                        if s == 0:
                            x_transpose(0, i + 1, 1, i, 0)
                            kv(i, 0, 2)
                        if s == 1:
                            kv(i, 5, 6)
                            ls_transpose(i)
                            kv(i, 6, 8)
                        if s == 2:
                            wo_half(i, 0, 3, 4)
                            wo_half(i, 1, 0, 1)
                        if s == 3:
                            wo_half(i, 0, 4, 7)
                        if s == 4:
                            q_half(i, 0, 0, 1)
                            wo_half(i, 0, 7, 8)
                        if s == 5:
                            q_half(i, 0, 3, 4)
                        if s == 6:
                            q_half(i, 1, 2, 3)
                        if s == 7:
                            q_half(i, 1, 6, 8)
                            k_transpose(i + 1, 1, i, 5)
                        p_transpose(*group(i, s - 1))
                        if s == 0:
                            kv(i, 2, 5)
                        if s == 1:
                            out_half(i, 0)
                            out_half(i, 1)
                        if s == 2:
                            wo_half(i, 1, 1, 2)
                        if s == 3:
                            wo_half(i, 1, 3, 4)
                        if s == 4:
                            wo_half(i, 1, 6, 7)
                            k_transpose(i + 1, 0, i, 2)
                            wo_half(i, 1, 7, 8)
                        if s == 5:
                            q_half(i, 0, 4, 6)
                        if s == 6:
                            x_transpose(1, i - 1, 0, i, 3)
                            q_half(i, 1, 3, 6)
                        if s == 7:
                            x_transpose(0, i + 2, 0, i, 6)
                            low(i, 0, 8)

                bodies(pe, body)

            @block.scalar
            def _(act):
                A = nc.scalar

                def copy_qt(b, g):
                    if not has(b):
                        return
                    reached(act, qt_done, G, b, g + 1)
                    pb_, pg = group(b, g - 2)
                    reached(act, s_done, G, pb_, pg + 1)
                    A.activation(qt[g % 2][:, :], tq[:, 0:HG * P], ACT.Copy).then_inc(qt_copied, 1)

                def exps(b, g):
                    if not has(b):
                        return
                    pb_, pg = group(b, g - 2)
                    reached(act, pt_done, G, pb_, pg + 1)
                    for j in range(HG):
                        reached(act, masked, 4 * G, b, 4 * g + j + 1)
                        last = A.activation(pr[g % 2][:, j * P:(j + 1) * P], sm[g % 2][:, j * P:(j + 1) * P], ACT.Exp,
                                            bias=smin[g % 2][:, j:j + 1], scale=-1.0,
                                            accum_out=rsum[g % 2][:, j:j + 1])
                    last.then_inc(exp_done, 1)

                def pt_high(b, g):
                    if not has(b):
                        return
                    reached(act, pt_done, G, b, g + 1)
                    A.activation(pt_hi[:, :], pt_ps[:, :], ACT.Copy).then_inc(pth_done, 1)

                def ctx_high(b, g):
                    if not has(b):
                        return
                    reached(act, pv_done, G, b, g + 1)
                    wo_free(act, b, g)
                    A.activation(ctx_hi[:, g, :], pv_ps[:, 0:P], ACT.Copy).then_inc(ctxh_done, 1)

                def norm_root(w, b):
                    if not has(b):
                        return
                    reached(act, ln_v[w], 8, b, 4)
                    A.activation(nrm[w][:, 1:2], nrm[w][:, 0:1], ACT.Ln).then_inc(ln_y[w], 1)
                    reached(act, ln_y[w], 2, b, 1)
                    A.activation(nrm[w][:, 2:3], nrm[w][:, 1:2], ACT.Exp, scale=-0.5).then_inc(ln_y[w], 1)

                def norm_apply(w, b):
                    if not has(b):
                        return
                    reached(act, ln_v[w], 8, b, 8)
                    reached(act, xt_done[w], 2, b)
                    A.activation(xn[w][:, :], (h_ln, h1)[w][:, :], ACT.Identity, bias=nrm[w][:, 6:7],
                                 scale=nrm[w][:, 5:6]).then_inc(ln_x[w], 1)

                def xt_high(w, b, tile):
                    if not has(b):
                        return
                    reached(act, xt_done[w], 2, b, tile + 1)
                    A.activation(xt_hi[w][:, 4 * tile:4 * tile + 4, :],
                                 tx[:, :].rearrange("p (k t) -> p k t", k=4), ACT.Copy).then_inc(xth_done[w], 1)

                def copy_kt_a(b):
                    if not has(b):
                        return
                    reached(act, kt_done, 2, b, 1)
                    A.activation(kt[:, 0:4, :], tx16[:, 0:4 * P].rearrange("p (k t) -> p k t", k=4),
                                 ACT.Copy).then_inc(kt_copied, 1)

                def q_high_b(b):
                    if not has(b):
                        return
                    reached(act, q_sum, 2, b, 2)
                    reached(act, qt_done, G, b - 1, 8)
                    A.activation(qs[:, 16:32, 0, 0, :], qr[:, :].rearrange("p (h d) -> p h d", d=HD),
                                 ACT.Copy).then_inc(qh_done, 1)

                def k_high(b):
                    if not has(b):
                        return
                    reached(act, k_sum, 1, b, 1)
                    reached(act, kt_done, 2, b)
                    A.activation(ks[:, :, 0, 0, :], kr[:, :].rearrange("p (h d) -> p h d", d=HD),
                                 ACT.Copy).then_inc(kh_done, 1)

                def v_high(b):
                    if not has(b):
                        return
                    reached(act, kv_used, 1, b, 1)
                    reached(act, pv_done, G, b)
                    A.activation(v_hi[:, :], vf[:, :], ACT.Copy).then_inc(vh_done, 1)

                def router_exp(b):
                    if not has(b):
                        return
                    reached(act, low_v, 5, b, 2)
                    A.activation(e8[:, :], z8[:, :], ACT.Exp, bias=s8[:, 0:1],
                                 accum_out=s8[:, 1:2]).then_inc(low_e, 1)

                def ls_high(b):
                    if not has(b):
                        return
                    reached(act, lst_done, 1, b, 1)
                    reached(act, out_done, 2, b)
                    A.activation(ls_hi[:, :], tx[:, 0:P], ACT.Copy).then_inc(lsh_done, 1)

                def body(i):
                    for s in range(G):
                        copy_qt(*group(i, s + 1))
                        if s == 0:
                            xt_high(0, i + 1, 1)
                        if s == 1:
                            ls_high(i - 2)
                            v_high(i)
                        if s == 4:
                            k_high(i + 1)
                            norm_root(0, i + 2)
                        exps(i, s)
                        ctx_high(*group(i, s - 2))
                        if s == 6:
                            xt_high(1, i - 1, 0)
                        pt_high(*group(i, s - 1))
                        if s == 0:
                            q_high_b(i)
                            router_exp(i - 2)
                        if s == 5:
                            norm_root(1, i - 1)
                            norm_apply(0, i + 2)
                            norm_apply(1, i - 1)
                            copy_kt_a(i + 1)
                        if s == 6:
                            xt_high(1, i - 1, 1)
                        if s == 7:
                            xt_high(0, i + 2, 0)

                A.preload_act_table_set("natural_log_exp_and_others")
                bodies(act, body)

            @block.vector
            def _(dve):
                V = nc.vector

                def mask_min(b, g):
                    if not has(b):
                        return
                    reached(dve, s_done, G, b, g + 1)
                    pb_, pg = group(b, g - 2)
                    reached(dve, exp_done, G, pb_, pg + 1)
                    hold_waits(dve)
                    for j in range(HG):
                        V.tensor_tensor_reduce(sm[g % 2][:, j * P:(j + 1) * P], s_ps[:, j * P:(j + 1) * P],
                                               mask, 1.0, 3e38, ALU.add, ALU.min,
                                               smin[g % 2][:, j:j + 1]).then_inc(masked, 1)

                def reciprocals(b, g):
                    if not has(b):
                        return
                    reached(dve, exp_done, G, b, g + 1)
                    V.reciprocal(rinv[g % 2][:, :], rsum[g % 2][:, :]).then_inc(rinv_done, 1)

                def pt_low(b, g):
                    if not has(b):
                        return
                    reached(dve, pth_done, G, b, g + 1)
                    V.tensor_tensor(pt_lo[:, :], pt_ps[:, :], pt_hi[:, :], ALU.subtract).then_inc(ptl_done, 1)

                def ctx_low(b, g):
                    if not has(b):
                        return
                    reached(dve, ctxh_done, G, b, g + 1)
                    V.tensor_tensor(ctx_lo[:, g, :], pv_ps[:, 0:P], ctx_hi[:, g, :], ALU.subtract).then_inc(ctxl_done, 1)

                def norm_half(w, src, b, half):
                    V.bn_stats(bn[w][:, 6 * half:6 * half + 6], src[:, 512 * half:512 * half + 512]).then_inc(ln_v[w], 1)

                def norm_stats(w, b):
                    reached(dve, ln_v[w], 8, b, 2)
                    hold_waits(dve)
                    V.bn_aggr(mv[w][:, :], bn[w][:, :]).then_inc(ln_v[w], 1)
                    reached(dve, ln_v[w], 8, b, 3)
                    V.tensor_scalar(nrm[w][:, 0:1], mv[w][:, 1:2], LN_EPS, None, ALU.add).then_inc(ln_v[w], 1)

                def norm_refine(w, b):
                    if not has(b):
                        return
                    v, y, a, c, scale, shift = (nrm[w][:, n:n + 1] for n in (0, 2, 3, 4, 5, 6))
                    reached(dve, ln_y[w], 2, b, 2)
                    V.scalar_tensor_tensor(a, y, v, y, ALU.mult, ALU.mult).then_inc(ln_v[w], 1)
                    reached(dve, ln_v[w], 8, b, 5)
                    V.tensor_scalar(c, a, -0.5, 1.5, ALU.mult, ALU.add).then_inc(ln_v[w], 1)
                    reached(dve, ln_v[w], 8, b, 6)
                    V.tensor_tensor(scale, y, c, ALU.mult).then_inc(ln_v[w], 1)
                    reached(dve, ln_v[w], 8, b, 7)
                    V.scalar_tensor_tensor(shift, mv[w][:, 0:1], -1.0, scale, ALU.mult, ALU.mult).then_inc(ln_v[w], 1)

                def norm1_stats(b):
                    if not has(b):
                        return
                    dve.wait_ge(ln_in, 16 * b + 16)
                    norm_half(0, h_ln, b, 0)
                    norm_half(0, h_ln, b, 1)
                    norm_stats(0, b)

                def xt_low(w, b, tile):
                    if not has(b):
                        return
                    reached(dve, xth_done[w], 2, b, tile + 1)
                    V.tensor_tensor(xt_lo[w][:, 4 * tile:4 * tile + 4, :], tx[:, :].rearrange("p (k t) -> p k t", k=4),
                                    xt_hi[w][:, 4 * tile:4 * tile + 4, :], ALU.subtract).then_inc(xtl_done[w], 1)

                def rotate(cos_part, sin_part, src, n, at_c, at_s):
                    x4 = src.rearrange("p (h a d) -> p h a d", h=n, a=2)
                    c = cst[:, at_c:at_c + HD].unsqueeze(1).broadcast_to([P, n, HD])
                    V.tensor_tensor(cos_part.rearrange("p (h d) -> p h d", d=HD),
                                    src.rearrange("p (h d) -> p h d", d=HD), c, ALU.mult)
                    y4 = sin_part.rearrange("p (h a d) -> p h a d", h=n, a=2)
                    for a in range(2):
                        sn = cst[:, at_s + a * HD // 2:at_s + (a + 1) * HD // 2]
                        last = V.tensor_tensor(y4[:, :, a, :], x4[:, :, 1 - a, :],
                                               sn.unsqueeze(1).broadcast_to([P, n, HD // 2]), ALU.mult)
                    return last

                def kv_rotate(b):
                    if not has(b):
                        return
                    reached(dve, kv_done, 1, b, 1)
                    reached(dve, vl_done, 1, b)
                    reached(dve, k_sum, 1, b)
                    V.tensor_scalar(vf[:, :], pa[:, G * HD:], INV_WS, None, ALU.mult)
                    rotate(kt_c[:, :], kt_s[:, :], pa[:, 0:G * HD], G, C_KC, C_KS).then_inc(kv_used, 1)

                def q_rotate(b, half):
                    if not has(b):
                        return
                    reached(dve, q_done, 2, b, half + 1)
                    reached(dve, q_sum, 2, b, half)
                    rotate(rt_c[:, :], rt_s[:, :], (pc, pa)[half][:, :], H // 2, C_QC, C_QS).then_inc(q_used, 1)

                def q_high_a(b):
                    if not has(b):
                        return
                    reached(dve, q_sum, 2, b, 1)
                    reached(dve, qt_done, G, b - 1, 4)
                    V.tensor_copy(qs[:, 0:16, 0, 0, :], qr[:, :].rearrange("p (h d) -> p h d", d=HD)).then_inc(qh_done, 1)

                def copy_kt_b(b):
                    if not has(b):
                        return
                    reached(dve, kt_done, 2, b, 2)
                    V.tensor_copy(kt[:, 4:8, :],
                                  tx16[:, 0:4 * P].rearrange("p (k t) -> p k t", k=4)).then_inc(kt_copied, 1)

                def q_double(b, half):
                    if not has(b):
                        return
                    reached(dve, qh_done, 2, b, half + 1)
                    reached(dve, ql_done, 2, b, half + 1)
                    part = qs[:, 16 * half:16 * half + 16, :, :, :].rearrange("p h a b d -> p h a (b d)")
                    V.tensor_copy(part[:, :, 1, :], part[:, :, 0, :]).then_inc(qd_done, 1)

                def k_double(b):
                    if not has(b):
                        return
                    reached(dve, kh_done, 1, b, 1)
                    reached(dve, kl_done, 1, b, 1)
                    part = ks[:, :, :, :, :].rearrange("p g a b d -> p (g a) b d")
                    V.tensor_copy(part[:, :, 1, :], part[:, :, 0, :]).then_inc(kd_done, 1)

                def residual1(b, half):
                    if not has(b):
                        return
                    reached(dve, wo_done, 2, b, half + 1)
                    dve.wait_ge(res_in, 16 * b + 16)
                    cols = slice(512 * half, 512 * half + 512)
                    V.scalar_tensor_tensor(h1[:, cols], (pa, pb)[half][:, :], INV_WS, h_res[:, cols],
                                           ALU.mult, ALU.add).then_inc(h1_done, 1)
                    reached(dve, h1_done, 2, b, half + 1)
                    norm_half(1, h1, b, half)
                    if half == 1:
                        norm_stats(1, b)

                def residual2(b, half):
                    if not has(b):
                        return
                    reached(dve, out_done, 2, b, half + 1)
                    if half == 0:
                        reached(dve, out_sent, 16, b)
                    cols = slice(512 * half, 512 * half + 512)
                    V.scalar_tensor_tensor(h2[:, cols], (pb, pc)[half][:, :], INV_WS, h1[:, cols],
                                           ALU.mult, ALU.add).then_inc(h2_done, 1)

                def router_max(b):
                    if not has(b):
                        return
                    reached(dve, low_done, 1, b, 1)
                    V.scalar_tensor_tensor(z8[:, :], pb[:, P:AW], INV_WS, W["br_all"][:, :],
                                           ALU.mult, ALU.add).then_inc(low_v, 1)
                    reached(dve, low_v, 5, b, 1)
                    V.tensor_reduce(s8[:, 0:1], z8[:, :], AX.X, ALU.max, negate=True).then_inc(low_v, 1)

                def router_weights(b):
                    if not has(b):
                        return
                    reached(dve, low_e, 1, b, 1)
                    V.reciprocal(s8[:, 2:3], s8[:, 1:2]).then_inc(low_v, 1)
                    reached(dve, low_v, 5, b, 3)
                    V.tensor_scalar(w8[:, :], e8[:, :], s8[:, 2:3], FFN_SCALE * INV_WS, ALU.mult, ALU.mult).then_inc(low_v, 1)
                    reached(dve, low_v, 5, b, 4)
                    V.tensor_tensor(ls[:, :].rearrange("p (h r) -> p h r", r=R),
                                    pb[:, 0:P].rearrange("p (h r) -> p h r", r=R),
                                    w8[:, :].unsqueeze(2).broadcast_to([P, NF, R]), ALU.mult).then_inc(low_v, 1)

                def ls_low(b):
                    if not has(b):
                        return
                    reached(dve, lsh_done, 1, b, 1)
                    V.tensor_tensor(ls_lo[:, :], tx[:, 0:P], ls_hi[:, :], ALU.subtract).then_inc(lsl_done, 1)

                def body(i):
                    for s in range(G):
                        if s == 0:
                            router_max(i - 2)
                        mask_min(i, s)
                        if s == 0:
                            xt_low(0, i + 1, 1)
                        if s == 1:
                            ls_low(i - 2)
                            kv_rotate(i + 1)
                            residual2(i - 2, 0)
                            q_double(i, 1)
                        if s == 2:
                            norm1_stats(i + 2)
                        if s == 4:
                            norm_refine(0, i + 2)
                            k_double(i + 1)
                        if s == 5:
                            residual1(i - 1, 1)
                        if s == 6:
                            q_rotate(i + 1, 0)
                            q_high_a(i + 1)
                        if s == 7:
                            xt_low(1, i - 1, 1)
                            copy_kt_b(i + 1)
                            q_rotate(i + 1, 1)
                        reciprocals(i, s)
                        if s == 1:
                            residual2(i - 2, 1)
                        if s == 5:
                            norm_refine(1, i - 1)
                        ctx_low(*group(i, s - 2))
                        if s == 6:
                            xt_low(1, i - 1, 0)
                        pt_low(*group(i, s - 1))
                        if s == 0:
                            router_weights(i - 2)
                        if s == 4:
                            residual1(i - 1, 0)
                        if s == 6:
                            q_double(i + 1, 0)
                        if s == 7:
                            xt_low(0, i + 2, 0)

                bodies(dve, body)

            @block.gpsimd
            def _(pool):
                def normalise(b, g):
                    if not has(b):
                        return
                    reached(pool, rinv_done, G, b, g + 1)
                    p3 = pr[g % 2][:, :].rearrange("p (j k) -> p j k", j=HG)
                    nc.gpsimd.tensor_tensor(p3, p3, rinv[g % 2][:, :].unsqueeze(2).broadcast_to([P, HG, P]),
                                            ALU.mult).then_inc(p_norm, 1)

                def sum_q(b, half):
                    if not has(b):
                        return
                    reached(pool, q_used, 2, b, half + 1)
                    pb_, ph = (b, 0) if half else (b - 1, 1)
                    reached(pool, qh_done, 2, pb_, ph + 1)
                    reached(pool, ql_done, 2, pb_, ph + 1)
                    nc.gpsimd.tensor_tensor(qr[:, :], rt_c[:, :], rt_s[:, :], ALU.add).then_inc(q_sum, 1)

                def q_low(b, half):
                    if not has(b):
                        return
                    reached(pool, qh_done, 2, b, half + 1)
                    part = qs[:, 16 * half:16 * half + 16, 0, :, :]
                    nc.gpsimd.tensor_tensor(part[:, :, 1, :], qr[:, :].rearrange("p (h d) -> p h d", d=HD),
                                            part[:, :, 0, :], ALU.subtract).then_inc(ql_done, 1)

                def sum_k(b):
                    if not has(b):
                        return
                    reached(pool, kv_used, 1, b, 1)
                    reached(pool, kh_done, 1, b)
                    reached(pool, kl_done, 1, b)
                    nc.gpsimd.tensor_tensor(kr[:, :], kt_c[:, :], kt_s[:, :], ALU.add).then_inc(k_sum, 1)

                def k_low(b):
                    if not has(b):
                        return
                    reached(pool, kh_done, 1, b, 1)
                    nc.gpsimd.tensor_tensor(ks[:, :, 1, 0, :], kr[:, :].rearrange("p (h d) -> p h d", d=HD),
                                            ks[:, :, 0, 0, :], ALU.subtract).then_inc(kl_done, 1)

                def v_low(b):
                    if not has(b):
                        return
                    reached(pool, vh_done, 1, b, 1)
                    nc.gpsimd.tensor_tensor(v_lo[:, :], vf[:, :], v_hi[:, :], ALU.subtract).then_inc(vl_done, 1)

                def body(i):
                    for s in range(G):
                        if s == 0:
                            sum_q(i, 1)
                        normalise(i, s)
                        if s == 0:
                            v_low(i)
                            q_low(i, 1)
                        if s == 2:
                            sum_k(i + 1)
                        if s == 3:
                            k_low(i + 1)
                        if s == 5:
                            sum_q(i + 1, 0)
                            q_low(i + 1, 0)

                bodies(pool, body)


_INS = ['x', 'L0_tok_log_dt', 'L0_tok_Lambda', 'L0_attn_Wq', 'L0_attn_Wk', 'L0_attn_Wv', 'L0_attn_Wo',
        'L0_ffn_A', 'L0_ffn_B', 'L0_ffn_Wr', 'L0_ffn_br']


def kernel(**inputs):
    import concourse.bacc as bacc
    from concourse.bass_utils import run_bass_kernel_spmd

    nc = bacc.Bacc("TRN2", target_bir_lowering=False, num_devices=1)
    arrays, args = {}, []
    for name in _INS:
        arrays[name] = np.ascontiguousarray(inputs[name])
        args.append(nc.dram_tensor(name, arrays[name].shape, f32, kind="ExternalInput").ap())
    arrays["consts"] = constants()
    args.append(nc.dram_tensor("consts", (P, C_N), f32, kind="ExternalInput").ap())
    h0 = nc.dram_tensor("h0", (NB, T, D), f32).ap()
    out = nc.dram_tensor("out", (NB, T, D), f32, kind="ExternalOutput").ap()
    x, log_dt, lam, wq, wk, wv, wo, fa, fb, wr, br, consts = args
    vit_layer(nc, x, log_dt, lam, wq, wk, wv, wo, fa, fb, wr, br, consts, h0, out)
    r = run_bass_kernel_spmd(nc, [arrays], core_ids=[0])
    return r.results[0]["out"]
```
